# Optimizing a Trainium2 kernel written in Bass

```python
import numpy as np
import jax
import jax.numpy as jnp

def _softmax(x, axis=-1):
    return jax.nn.softmax(x, axis=axis)

def _gelu(x):
    return jax.nn.gelu(x, approximate=True)

def _silu(x):
    return jax.nn.silu(x)

def _sigmoid(x):
    return jax.nn.sigmoid(x)

def _layernorm(x, axis=-1, eps=1e-05):
    m = jnp.mean(x, axis=axis, keepdims=True)
    v = jnp.var(x, axis=axis, keepdims=True)
    return (x - m) / jnp.sqrt(v + eps)

def _scatter_add(tgt, idx, src, axis=0):
    return tgt.at[idx].add(src)

def _segment_sum(src, seg, n):
    return jax.ops.segment_sum(src, seg, n)
kernel_name = 'mk_adaln_d1_jaxref_r8_165f82'

def setup_inputs(seed: int=0):
    np.random.seed(seed)
    _w = jnp.asarray

    def _L0_attn_setup():
        import jax, jax.numpy as jnp
        import numpy as np
        L, B, S, D, H, HID = (6, 4, 128, 128, 16, 512)
        HD = D // H

        def _pos_encoding(S, D):
            pos = np.arange(S)
            level = np.frexp((pos + 1).astype(np.float64))[1] - 1
            coord = (pos >> level) / 2.0 ** level
            div = np.exp(np.arange(0, D, 2, dtype=np.float64) * -(np.log(10000.0) / D))
            ang = pos[:, None].astype(np.float64) * div[None, :]
            pe = np.zeros((S, D), np.float32)
            pe[:, 0::2] = (np.sin(ang) * coord[:, None]).astype(np.float32)
            pe[:, 1::2] = (np.cos(ang) * coord[:, None]).astype(np.float32)
            return jnp.asarray(pe)

        def _sierpinski_mask(S):
            i = np.arange(S)
            return jnp.asarray((np.bitwise_and(i[:, None], i[None, :]) == 0).astype(np.float32))

        def _ln(h, g, b, eps=1e-05):
            m = h.mean(-1, keepdims=True)
            v = h.var(-1, keepdims=True)
            return (h - m) * jax.lax.rsqrt(v + eps) * g + b
        key = jax.random.key(seed)
        ks = iter(jax.random.split(key, 16))
        w = lambda k, shape: 0.02 * jax.random.normal(k, shape, jnp.float32)
        return {'x': jax.random.normal(next(ks), (B, S, D), jnp.float32), 'Wq': w(next(ks), (L, D, D)), 'bq': jnp.zeros((L, D), jnp.float32), 'Wk': w(next(ks), (L, D, D)), 'bk': jnp.zeros((L, D), jnp.float32), 'Wv': w(next(ks), (L, D, D)), 'bv': jnp.zeros((L, D), jnp.float32), 'Wo': w(next(ks), (L, D, D)), 'bo': jnp.zeros((L, D), jnp.float32), 'W1': w(next(ks), (L, D, HID)), 'b1': jnp.zeros((L, HID), jnp.float32), 'W2': w(next(ks), (L, HID, D)), 'b2': jnp.zeros((L, D), jnp.float32), 'ln1_g': jnp.ones((L, D), jnp.float32), 'ln1_b': jnp.zeros((L, D), jnp.float32), 'ln2_g': jnp.ones((L, D), jnp.float32), 'ln2_b': jnp.zeros((L, D), jnp.float32), 'lnf_g': jnp.ones((D,), jnp.float32), 'lnf_b': jnp.zeros((D,), jnp.float32)}
    _L0_attn_in = _L0_attn_setup()

    def _L0_ffn_setup():
        import jax, jax.numpy as jnp
        import numpy as np
        B, S, H = (2, 128, 128)
        E, F = (16, 64)
        G, TOPK_G, TOPK = (4, 2, 4)
        N_SHARED = 2
        ROUTE_SCALE = 1.0
        FS = N_SHARED * F

        def _gate(x, w_gate):
            T = x.shape[0]
            scores = jax.nn.sigmoid(x @ w_gate.T)
            sv = scores.reshape(T, G, E // G)
            group_scores = jax.lax.top_k(sv, 2)[0].sum(-1)
            top_groups = jax.lax.top_k(group_scores, TOPK_G)[1]
            allowed = jnp.zeros((T, G), dtype=bool).at[jnp.arange(T)[:, None], top_groups].set(True)
            masked = jnp.where(allowed[:, :, None], sv, -jnp.inf).reshape(T, E)
            _, idx = jax.lax.top_k(masked, TOPK)
            w = jnp.take_along_axis(scores, idx, axis=1)
            w = w / (w.sum(-1, keepdims=True) + 1e-06) * ROUTE_SCALE
            return (w, idx)

        def _swiglu(x, w1, w3, w2):
            return jax.nn.silu(x @ w1.T) * (x @ w3.T) @ w2.T
        key = jax.random.key(seed)
        ks = jax.random.split(key, 8)
        scale = 0.02
        return {'hidden_states': jax.random.normal(ks[0], (B, S, H), dtype=jnp.float32), 'w_gate': jax.random.normal(ks[1], (E, H), dtype=jnp.float32) * scale, 'w1_e': jax.random.normal(ks[2], (E, F, H), dtype=jnp.float32) * scale, 'w3_e': jax.random.normal(ks[3], (E, F, H), dtype=jnp.float32) * scale, 'w2_e': jax.random.normal(ks[4], (E, H, F), dtype=jnp.float32) * scale, 'w1_s': jax.random.normal(ks[5], (FS, H), dtype=jnp.float32) * scale, 'w3_s': jax.random.normal(ks[6], (FS, H), dtype=jnp.float32) * scale, 'w2_s': jax.random.normal(ks[7], (H, FS), dtype=jnp.float32) * scale}
    _L0_ffn_in = _L0_ffn_setup()
    _L0_c = _w((lambda *s: np.random.randn(*s).astype(np.float32) * 0.05)(4, 128))
    _L0_wmod = _w((lambda *s: np.random.randn(*s).astype(np.float32) * 0.05)(128, 6 * 128) * 128 ** (-0.5))
    _d = {'L0_attn_x': _L0_attn_in['x'], 'L0_attn_Wq': _L0_attn_in['Wq'], 'L0_attn_bq': _L0_attn_in['bq'], 'L0_attn_Wk': _L0_attn_in['Wk'], 'L0_attn_bk': _L0_attn_in['bk'], 'L0_attn_Wv': _L0_attn_in['Wv'], 'L0_attn_bv': _L0_attn_in['bv'], 'L0_attn_Wo': _L0_attn_in['Wo'], 'L0_attn_bo': _L0_attn_in['bo'], 'L0_attn_W1': _L0_attn_in['W1'], 'L0_attn_b1': _L0_attn_in['b1'], 'L0_attn_W2': _L0_attn_in['W2'], 'L0_attn_b2': _L0_attn_in['b2'], 'L0_attn_ln1_g': _L0_attn_in['ln1_g'], 'L0_attn_ln1_b': _L0_attn_in['ln1_b'], 'L0_attn_ln2_g': _L0_attn_in['ln2_g'], 'L0_attn_ln2_b': _L0_attn_in['ln2_b'], 'L0_attn_lnf_g': _L0_attn_in['lnf_g'], 'L0_attn_lnf_b': _L0_attn_in['lnf_b'], 'L0_ffn_w_gate': _L0_ffn_in['w_gate'], 'L0_ffn_w1_e': _L0_ffn_in['w1_e'], 'L0_ffn_w3_e': _L0_ffn_in['w3_e'], 'L0_ffn_w2_e': _L0_ffn_in['w2_e'], 'L0_ffn_w1_s': _L0_ffn_in['w1_s'], 'L0_ffn_w3_s': _L0_ffn_in['w3_s'], 'L0_ffn_w2_s': _L0_ffn_in['w2_s'], 'L0_c': _L0_c, 'L0_wmod': _L0_wmod}
    _x0 = _d['L0_attn_x']
    _d['L0_attn_x'] = jax.random.normal(jax.random.fold_in(jax.random.key(seed), 1), (4, 1024, 128), dtype=_x0.dtype)
    del _x0
    return _d

def reference(L0_attn_x, L0_attn_Wq, L0_attn_bq, L0_attn_Wk, L0_attn_bk, L0_attn_Wv, L0_attn_bv, L0_attn_Wo, L0_attn_bo, L0_attn_W1, L0_attn_b1, L0_attn_W2, L0_attn_b2, L0_attn_ln1_g, L0_attn_ln1_b, L0_attn_ln2_g, L0_attn_ln2_b, L0_attn_lnf_g, L0_attn_lnf_b, L0_ffn_w_gate, L0_ffn_w1_e, L0_ffn_w3_e, L0_ffn_w2_e, L0_ffn_w1_s, L0_ffn_w3_s, L0_ffn_w2_s, L0_c, L0_wmod):

    def _L0_attn_ref(x, Wq, bq, Wk, bk, Wv, bv, Wo, bo, W1, b1, W2, b2, ln1_g, ln1_b, ln2_g, ln2_b, lnf_g, lnf_b):
        import jax, jax.numpy as jnp
        import numpy as np
        L, B, S, D, H, HID = (6, 4, 128, 128, 16, 512)
        HD = D // H

        def _pos_encoding(S, D):
            pos = np.arange(S)
            level = np.frexp((pos + 1).astype(np.float64))[1] - 1
            coord = (pos >> level) / 2.0 ** level
            div = np.exp(np.arange(0, D, 2, dtype=np.float64) * -(np.log(10000.0) / D))
            ang = pos[:, None].astype(np.float64) * div[None, :]
            pe = np.zeros((S, D), np.float32)
            pe[:, 0::2] = (np.sin(ang) * coord[:, None]).astype(np.float32)
            pe[:, 1::2] = (np.cos(ang) * coord[:, None]).astype(np.float32)
            return jnp.asarray(pe)

        def _sierpinski_mask(S):
            i = np.arange(S)
            return jnp.asarray((np.bitwise_and(i[:, None], i[None, :]) == 0).astype(np.float32))

        def _ln(h, g, b, eps=1e-05):
            m = h.mean(-1, keepdims=True)
            v = h.var(-1, keepdims=True)
            return (h - m) * jax.lax.rsqrt(v + eps) * g + b
        Bx, Sx, Dx = x.shape
        smask = _sierpinski_mask(Sx)
        h = x + _pos_encoding(Sx, Dx)
        scale = 1.0 / jnp.sqrt(jnp.float32(HD))

        def layer(h, p):
            wq, bq_, wk, bk_, wv, bv_, wo, bo_, w1, b1_, w2, b2_, g1, be1, g2, be2 = p
            q = (h @ wq + bq_).reshape(Bx, Sx, H, HD).transpose(0, 2, 1, 3)
            k = (h @ wk + bk_).reshape(Bx, Sx, H, HD).transpose(0, 2, 1, 3)
            v = (h @ wv + bv_).reshape(Bx, Sx, H, HD).transpose(0, 2, 1, 3)
            scores = jnp.einsum('bhqd,bhkd->bhqk', q, k) * scale
            scores = scores * smask
            a = jax.nn.softmax(scores, axis=-1)
            att = jnp.einsum('bhqk,bhkd->bhqd', a, v)
            att = att.transpose(0, 2, 1, 3).reshape(Bx, Sx, Dx) @ wo + bo_
            h = _ln(h + att, g1, be1)
            ff = jax.nn.gelu(h @ w1 + b1_, approximate=False) @ w2 + b2_
            h = _ln(h + ff, g2, be2)
            return (h, None)
        params = (Wq, bq, Wk, bk, Wv, bv, Wo, bo, W1, b1, W2, b2, ln1_g, ln1_b, ln2_g, ln2_b)
        h, _ = jax.lax.scan(layer, h, params)
        return _ln(h, lnf_g, lnf_b)

    def _L0_ffn_ref(hidden_states, w_gate, w1_e, w3_e, w2_e, w1_s, w3_s, w2_s):
        import jax, jax.numpy as jnp
        import numpy as np
        B, S, H = (2, 128, 128)
        E, F = (16, 64)
        G, TOPK_G, TOPK = (4, 2, 4)
        N_SHARED = 2
        ROUTE_SCALE = 1.0
        FS = N_SHARED * F

        def _gate(x, w_gate):
            T = x.shape[0]
            scores = jax.nn.sigmoid(x @ w_gate.T)
            sv = scores.reshape(T, G, E // G)
            group_scores = jax.lax.top_k(sv, 2)[0].sum(-1)
            top_groups = jax.lax.top_k(group_scores, TOPK_G)[1]
            allowed = jnp.zeros((T, G), dtype=bool).at[jnp.arange(T)[:, None], top_groups].set(True)
            masked = jnp.where(allowed[:, :, None], sv, -jnp.inf).reshape(T, E)
            _, idx = jax.lax.top_k(masked, TOPK)
            w = jnp.take_along_axis(scores, idx, axis=1)
            w = w / (w.sum(-1, keepdims=True) + 1e-06) * ROUTE_SCALE
            return (w, idx)

        def _swiglu(x, w1, w3, w2):
            return jax.nn.silu(x @ w1.T) * (x @ w3.T) @ w2.T
        shape = hidden_states.shape
        x = hidden_states.reshape(-1, H)
        weights, idx = _gate(x, w_gate)
        combine = (jax.nn.one_hot(idx, E, dtype=x.dtype) * weights[..., None]).sum(1)
        g = jax.nn.silu(jnp.einsum('th,efh->tef', x, w1_e))
        u = jnp.einsum('th,efh->tef', x, w3_e)
        routed = jnp.einsum('tef,ehf,te->th', g * u, w2_e, combine)
        shared = _swiglu(x, w1_s, w3_s, w2_s)
        return (routed + shared).reshape(shape)
    x = L0_attn_x
    mod = (_silu(L0_c) @ L0_wmod).reshape(L0_c.shape[0], 6, 1, -1)
    sa, ca, ga, sb, cb, gb = (mod[:, 0], mod[:, 1], mod[:, 2], mod[:, 3], mod[:, 4], mod[:, 5])
    ga = (2 * (ga >= 0) - 1) * jnp.maximum(jnp.abs(ga), 0.25)
    gb = (2 * (gb >= 0) - 1) * jnp.maximum(jnp.abs(gb), 0.25)
    h = _layernorm(x, axis=-1) * (1 + ca) + sa
    x = x + ga * _L0_attn_ref(h, L0_attn_Wq, L0_attn_bq, L0_attn_Wk, L0_attn_bk, L0_attn_Wv, L0_attn_bv, L0_attn_Wo, L0_attn_bo, L0_attn_W1, L0_attn_b1, L0_attn_W2, L0_attn_b2, L0_attn_ln1_g, L0_attn_ln1_b, L0_attn_ln2_g, L0_attn_ln2_b, L0_attn_lnf_g, L0_attn_lnf_b)
    h = _layernorm(x, axis=-1) * (1 + cb) + sb
    x = x + gb * _L0_ffn_ref(h, L0_ffn_w_gate, L0_ffn_w1_e, L0_ffn_w3_e, L0_ffn_w2_e, L0_ffn_w1_s, L0_ffn_w3_s, L0_ffn_w2_s)
    return x

_drawn_inputs = setup_inputs


def setup_inputs(seed=0):
    import zlib

    import numpy as np

    out = dict(_drawn_inputs(seed))
    spreads = {'L0_attn_bq': (0.0, 0.8),
     'L0_attn_bk': (0.0, 0.8),
     'L0_attn_bv': (0.0, 0.701),
     'L0_attn_bo': (0.0, 0.1),
     'L0_attn_b1': (0.0, 0.541),
     'L0_attn_b2': (0.0, 0.1),
     'L0_attn_ln1_g': (1.0, 0.2),
     'L0_attn_ln1_b': (0.0, 0.1),
     'L0_attn_ln2_g': (1.0, 0.2),
     'L0_attn_ln2_b': (0.0, 0.1),
     'L0_attn_lnf_g': (1.0, 0.2),
     'L0_attn_lnf_b': (0.0, 0.316)}
    factors = {'L0_attn_Wq': 8.0,
     'L0_attn_Wk': 8.0,
     'L0_attn_Wv': 6.314,
     'L0_attn_Wo': 4.778,
     'L0_ffn_w_gate': 8.0,
     'L0_ffn_w1_e': 8.0,
     'L0_ffn_w3_e': 8.0,
     'L0_ffn_w2_e': 8.0,
     'L0_ffn_w1_s': 8.0,
     'L0_ffn_w3_s': 8.0,
     'L0_ffn_w2_s': 8.0}
    for name, (base, spread) in spreads.items():
        noise = np.random.default_rng([zlib.crc32(name.encode()), seed]).standard_normal(out[name].shape)
        drawn = base * np.exp(spread * noise) if base else spread * noise
        out[name] = jnp.asarray(drawn.astype(out[name].dtype))
    for name, factor in factors.items():
        out[name] = (out[name] * factor).astype(out[name].dtype)
    return out
```

```python
from contextlib import ExitStack

import concourse.bass as bass
from concourse import mybir

F32 = mybir.dt.float32
ALU = mybir.AluOpType
ACT = mybir.ActivationFunctionType
AX_X = mybir.AxisListType.X

LAYERS, BATCH, SEQ, D, HEADS, HID = 6, 4, 1024, 128, 16, 512
HD = D // HEADS
LO = 8
BITS = 7
BLOCKS = SEQ // LO
HALF = SEQ // 2
ITERS = LAYERS * BATCH
FCH = HID // D
EPS = 1e-5
NEG = -1e30
SCALE = float(1.0 / (HD ** 0.5))
EXPERTS, GROUPS, EF = 16, 4, 64
MCH = 9
TILES = BATCH * SEQ // 128


def key_order():
    def by_size(j):
        return (bin(j).count("1"), j)
    return sorted(range(BLOCKS // 2), key=by_size), sorted(range(BLOCKS // 2, BLOCKS), key=by_size)


def placement():
    low, high = key_order()
    out, col = [], 0
    for js in (low, high):
        col = (col + HALF - 1) // HALF * HALF
        for j in js:
            n = LO << (BITS - bin(j).count("1"))
            out.append((j, col, n))
            col += n
    return out, col


PLACE, SCORE_COLS = placement()
UNIT = 2 * HALF
SUNITS = (SCORE_COLS + UNIT - 1) // UNIT
GAP = (sum(n for j, _, n in PLACE if j < BLOCKS // 2),
       [c for j, c, _ in PLACE if j == BLOCKS // 2][0])


def pieces(j, n, fixed_top=None, max_runs=2):
    held = {}
    if fixed_top is not None:
        if j >> (BITS - 1) & 1:
            if fixed_top:
                return
        held[BITS - 1] = fixed_top

    def runs(held):
        out = []
        for k in range(BITS - 1, -1, -1):
            kind = "fix" if (j >> k & 1 or k in held) else "free"
            val = held.get(k, 0)
            if out and out[-1][0] == kind and kind == "free":
                out[-1][1] += 1
            elif out and out[-1][0] == kind:
                out[-1] = [kind, out[-1][1] + 1, out[-1][2] * 2 + val]
            else:
                out.append([kind, 1, val])
        return out

    def strided(rs):
        free = [r for r in rs if r[0] == "free"]
        return len(free) - (1 if rs[-1][0] == "free" else 0)

    def split(held):
        rs = runs(held)
        if strided(rs) <= max_runs:
            off = 0
            for k, v in held.items():
                if v:
                    below = sum(1 for q in range(k) if not j >> q & 1)
                    off += LO << below
            cols = LO
            for r in rs:
                if r[0] == "free":
                    cols <<= r[1]
            yield off, cols, rs
            return
        top = max(k for k in range(BITS) if not j >> k & 1 and k not in held)
        yield from split({**held, top: 0})
        yield from split({**held, top: 1})

    yield from split(held)


def view_queries(ap, rs):
    names, sizes, index = [], {}, [slice(None)]
    for q, (kind, bits, val) in enumerate(rs):
        names.append(f"r{q}")
        sizes[f"r{q}"] = 1 << bits
        index.append(slice(None) if kind == "free" else val)
    v = ap.rearrange("p (" + " ".join(names) + " l) -> p " + " ".join(names) + " l", l=LO, **sizes)
    return v[tuple(index) + (slice(None),)]


def view_block(ap, rs):
    free = [(f"r{q}", 1 << bits) for q, (kind, bits, _) in enumerate(rs) if kind == "free"]
    names = " ".join(n for n, _ in free)
    return ap.rearrange(f"p ({names} l) -> p {names} l", l=LO, **dict(free))


def adaln_kernel(nc, x_t, pe_t, wa, wb, lnf, c_t, wmod, w_gate, we1, we3, we2,
                 ident_c, ones_c, mean_c, neg_c, cnt_c, floor_c, tri_c, ind_c,
                 h_dram, v_dram, out):
    with ExitStack() as ctx:
        def sb(name, shape):
            return ctx.enter_context(nc.sbuf_tensor(name, shape, F32))

        def sem(name):
            return ctx.enter_context(nc.semaphore(name))

        ring = ctx.enter_context(nc.psum_tensor("ring", [128, 2, UNIT], F32))
        acc = ctx.enter_context(nc.psum_tensor("acc", [128, SEQ], F32))
        red = ctx.enter_context(nc.psum_tensor("red", [128, SEQ], F32))

        diag = sb("diag", [128, 3, 128, BLOCKS // 2])
        score = sb("score", [128, SCORE_COLS])
        h_in = sb("h_in", [128, SEQ])
        q_t = sb("q_t", [128, SEQ])
        k_t = sb("k_t", [128, SEQ])
        tmp = sb("tmp", [128, 4, SEQ])
        n_t = tmp[:, 0, :]
        n_rev = tmp[:, 1, :]
        e0 = tmp[:, 2, :]
        den = tmp[:, 3, :]
        gl = tmp[:, :, :].rearrange("p a n -> p (a n)").rearrange("p (t c n) -> p t c n", t=2, c=FCH)
        h_sq = tmp[:, 0, :]
        wa_s = sb("wa_s", [128, 3 * D + 3])
        wb_s = sb("wb_s", [128, D + 2 * HID + 6 + FCH])
        ident = sb("ident", [128, 128])
        ones_b = sb("ones_b", [128, 128])
        mean_w = sb("mean_w", [128, 128])
        neg = sb("neg", [128, LO])
        cnt = sb("cnt", [128, SEQ])
        floor = sb("floor", [128, 1])
        m_tok = sb("m_tok", [128, BLOCKS])
        mod = sb("mod", [128, 6, BATCH])
        cur = sb("cur", [128, 6])
        lnf_s = sb("lnf_s", [128, 2])
        eps = sb("eps", [128, 1])
        one = sb("one", [128, 1])

        bq, bk, bv = (wa_s[:, 3 * D + i:3 * D + i + 1] for i in range(3))
        wo = wb_s[:, 0:D]
        w1 = wb_s[:, D:D + HID].rearrange("p (c n) -> p c n", c=FCH)
        w2 = wb_s[:, D + HID:D + 2 * HID].rearrange("p (c n) -> p c n", c=FCH)
        vec = D + 2 * HID
        bo, b2, g1, be1, g2, be2 = (wb_s[:, vec + i:vec + i + 1] for i in range(6))
        b1 = [wb_s[:, vec + 6 + c:vec + 7 + c] for c in range(FCH)]

        s_wmod = score[:, 0:6 * D].rearrange("p (m n) -> p m n", m=6)
        s_c = score[:, 6 * D:6 * D + BATCH]
        s_sig = score[:, 6 * D + BATCH:6 * D + 2 * BATCH]
        s_sgn = score[:, 6 * D + 2 * BATCH:6 * D + 4 * BATCH]
        s_pe_view = score[:, 2 * UNIT:3 * UNIT]
        hm = score[:, 0:4 * SEQ]
        x2 = score[:, 4 * SEQ:8 * SEQ]
        m_g = score[:, 8 * SEQ:8 * SEQ + 512]
        m_a = score[:, 8 * SEQ + 512:9 * SEQ]
        m_b = score[:, 9 * SEQ:9 * SEQ + 512]
        m_gs = score[:, 9 * SEQ + 512:9 * SEQ + 640]
        m_al = score[:, 9 * SEQ + 640:9 * SEQ + 768]
        m_t = [score[:, 9 * SEQ + 768 + 128 * i:9 * SEQ + 896 + 128 * i] for i in range(4)]
        m_rep = score[:, 10 * SEQ + 512:11 * SEQ]
        comb_t = score[0:EXPERTS, 11 * SEQ:15 * SEQ]
        out_s = score[:, 15 * SEQ:15 * SEQ + 2 * HALF].rearrange("p (a n) -> p a n", a=2)
        m_sg = score[:, 16 * SEQ:17 * SEQ].rearrange("p (a n) -> p a n", a=2)
        dflat = diag[:, :, :, :].rearrange("p a m j -> p (a m j)")
        m_c1 = dflat[:, 0:8192]
        m_c2 = dflat[:, 8192:16384]
        o = 16384
        e_w1 = dflat[:, o:o + MCH * 128].rearrange("p (c n) -> p c n", c=MCH)
        e_w3 = dflat[:, o + 1152:o + 2304].rearrange("p (c n) -> p c n", c=MCH)
        e_w2 = dflat[:, o + 2304:o + 3456].rearrange("p (c n) -> p c n", c=MCH)
        e_wg = dflat[:, o + 3456:o + 3472]
        e_tri = dflat[:, o + 3472:o + 3728].rearrange("p (a b) -> p a b", a=16)
        e_ind = dflat[0:EXPERTS, o + 3728:o + 4752].rearrange("p (c n) -> p c n", c=8)
        m_y = dflat[:, o + 4752:o + 5776].rearrange("p (a n) -> p a n", a=2)
        m_z = dflat[:, o + 5776:o + 6800].rearrange("p (a n) -> p a n", a=2)

        s_const = sem("const_loaded")
        s_zero = sem("diag_zeroed")
        s_eps = sem("eps_written")
        s_modw = sem("mod_weights_loaded")
        s_silu_e = sem("silu_exp_ready")
        s_silu = sem("silu_ready")
        s_dv = sem("vector_chain")
        s_modp = sem("mod_product_ready")
        s_modv = sem("mod_vector_steps")
        s_x = sem("x_loaded")
        s_cur = sem("mod_column_copied")
        s_pe = sem("pos_added")
        s_hst = sem("h_stored")
        s_h = sem("h_loaded")
        s_wa = sem("projection_weights_loaded")
        s_wb = sem("ffn_weights_loaded")
        s_full = sem("ring_unit_filled")
        s_free = sem("ring_unit_drained")
        s_vst = sem("v_stored")
        s_kx = sem("diag_keys_loaded")
        s_vx0 = sem("diag_values_low_loaded")
        s_vx1 = sem("diag_values_high_loaded")
        s_sdone = sem("score_halves_done")
        s_max = sem("max_steps")
        s_rtr = sem("maxima_transposed")
        s_m = sem("row_max_steps")
        s_mb = sem("row_max_spread")
        s_e0 = sem("exp_neg_max_ready")
        s_b = sem("shift_ready")
        s_shift = sem("score_unit_shifted")
        s_exp = sem("score_unit_exp")
        s_den = sem("den_steps")
        s_z = sem("subset_sum_steps")
        s_ec = sem("masked_terms_ready")
        s_pv = sem("pv_done")
        s_denb = sem("den_spread")
        s_fin = sem("attention_norm_steps")
        s_op = sem("out_projection_ready")
        s_lin = sem("ln_input_ready")
        s_lmean = sem("ln_mean_ready")
        s_lcen = sem("ln_centred")
        s_lsq = sem("ln_squared")
        s_lvar = sem("ln_variance_ready")
        s_lln = sem("ln_log_ready")
        s_lstd = sem("ln_rstd_ready")
        s_lnorm = sem("ln_normed")
        s_lout = sem("ln_output_ready")
        s_gelu = sem("gelu_ready")
        s_w1 = sem("ffn_up_done")
        s_w2 = sem("ffn_down_ready")
        s_x2 = sem("residual_ready")
        s_x2st = sem("residual_copied")
        s_gate = sem("gate_product_ready")
        s_gexp = sem("gate_exp_ready")
        s_gv = sem("gate_vector_steps")
        s_ctp = sem("combine_transposed")
        s_ctc = sem("combine_copied")
        s_gu = sem("expert_up_ready")
        s_cb = sem("combine_spread")
        s_sg = sem("expert_silu_ready")
        s_act = sem("expert_hidden_ready")
        s_hvs = sem("expert_hidden_steps")
        s_eo = sem("expert_out_ready")
        s_od = sem("expert_out_copied")
        s_out = sem("out_stored")
        ONE = 1
        STARTED = (s_vst, s_lout, s_pv, s_pe, s_hst, s_free, s_x2, s_act, s_od, s_out)
        block = ctx.enter_context(nc.Block())

        MOD_STEPS, GATE_STEPS = 4, 1
        PRE_LN, ITER_LN = 2 * BATCH, 4
        K_U, Q_U, V_U = (0, 1), (2,), (3,)
        S_U = 4
        G_U = S_U + SUNITS
        RING = G_U + 4
        assert RING % 2 == 0 and UNIT == SEQ

        def unit_spans(u):
            out = []
            for _, col, n in in_unit(u):
                if out and out[-1][1] == col - u * UNIT:
                    out[-1][1] += n
                else:
                    out.append([col - u * UNIT, col - u * UNIT + n])
            return out

        def chain(engine, signal, start=0):
            done = [start]

            def step(ins):
                ins.then_inc(signal, 1)
                done[0] += 1
                engine.wait_ge(signal, done[0])
            step.count = done
            return step

        def units_of_half(half):
            return [p for p in PLACE if (p[0] >= BLOCKS // 2) == half]

        def in_unit(u):
            return [p for p in PLACE if u * UNIT <= p[1] < (u + 1) * UNIT]

        MAXP = [(u, col, off, n, rs) for u in range(SUNITS) for j, col, nj in in_unit(u)
                for off, n, rs in pieces(j, nj)]
        NMAX = len(MAXP)

        @block.sync
        def _(sp):
            for s in STARTED:
                sp.sem_inc(s, ONE)
            for dst, src in ((ident, ident_c), (ones_b, ones_c), (mean_w, mean_c), (neg, neg_c), (cnt, cnt_c),
                             (floor, floor_c), (lnf_s, lnf)):
                sp.dma_start(dst[:], src).then_inc(s_const, 16)
            sp.dma_start(s_c, c_t).then_inc(s_modw, 16)
            sp.dma_start(s_wmod, wmod.rearrange("p (m n) -> p m n", m=6)).then_inc(s_modw, 16)
            sp.dma_start(s_pe_view, pe_t).then_inc(s_modw, 16)
            with sp.Fori(0, BATCH) as b:
                sp.wait_ge(s_pe, ONE + b * 2)
                sp.dma_start(h_in[:], x_t[bass.ds(b, 1)].rearrange("a p n -> p (a n)")).then_inc(s_x, 16)
                sp.wait_ge(s_pe, ONE + b * 2 + 2)
                sp.dma_start(h_dram[bass.ds(b, 1)].rearrange("a p n -> p (a n)"), q_t[:]).then_inc(s_hst, 16)
            sp.wait_ge(s_hst, ONE + 16 * BATCH)
            with sp.Fori(0, LAYERS) as l:
                with sp.Fori(0, BATCH) as b:
                    it = l * BATCH + b
                    sp.wait_ge(s_vst, ONE + it * 16)
                    sp.dma_start(wa_s[:], wa[bass.ds(l, 1)].rearrange("a p n -> p (a n)")).then_inc(s_wa, 16)
                    sp.wait_ge(s_hst, ONE + it * 16 + 16)
                    sp.wait_ge(s_lcen, it * ITER_LN + PRE_LN - 2)
                    sp.dma_start(h_in[:], h_dram[bass.ds(b, 1)].rearrange("a p n -> p (a n)")).then_inc(s_h, 16)
                    sp.wait_ge(s_lout, ONE + it * ITER_LN + PRE_LN)
                    sp.dma_start(wb_s[:], wb[bass.ds(l, 1)].rearrange("a p n -> p (a n)")).then_inc(s_wb, 16)
                    sp.wait_ge(s_zero, 3)
                    sp.wait_ge(s_pv, ONE + it)
                    sp.wait_ge(s_free, ONE + it * RING + K_U[1] + 1)
                    for h in range(HEADS):
                        p = slice(h * HD, (h + 1) * HD)
                        sp.dma_start(diag[p, 0:2, h * LO:(h + 1) * LO, :],
                                     k_t[p, :].rearrange("p (a l j) -> p a l j", a=2, l=LO)).then_inc(s_kx, 16)
                    sp.wait_ge(s_free, ONE + it * RING + V_U[0] + 1)
                    sp.dma_start(v_dram, n_t).then_inc(s_vst, 16)
                    sp.wait_ge(s_vst, ONE + it * 16 + 16)
                    for half, slot, s in ((0, 2, s_vx0), (1, 0, s_vx1)):
                        if half:
                            sp.wait_ge(s_sdone, it + 1)
                        for h in range(HEADS):
                            src = v_dram[h * HD:(h + 1) * HD, :].rearrange("d (l j) -> l d j", l=LO)
                            sp.dma_start(diag[h * LO:(h + 1) * LO, slot, h * HD:(h + 1) * HD, :],
                                         src[:, :, half * BLOCKS // 2:(half + 1) * BLOCKS // 2]).then_inc(s, 16)
            sp.wait_ge(s_hst, ONE + 16 * (BATCH + ITERS))
            for dst, src in ((e_w1, we1), (e_w3, we3), (e_w2, we2), (e_tri, tri_c), (e_ind, ind_c)):
                sp.dma_start(dst, src).then_inc(s_modw, 16)
            sp.dma_start(e_wg, w_gate).then_inc(s_modw, 16)
            with sp.Fori(0, BATCH) as b:
                sp.wait_ge(s_x2, ONE + b * 2)
                sp.dma_start(h_in[:], h_dram[bass.ds(b, 1)].rearrange("a p n -> p (a n)")).then_inc(s_h, 16)
                sp.dma_start(x2[:, bass.ds(b * SEQ, SEQ)], x_t[bass.ds(b, 1)].rearrange("a p n -> p (a n)"))\
                    .then_inc(s_x, 16)
            with sp.Fori(0, BATCH) as b:
                for t in range(2):
                    sp.wait_ge(s_od, ONE + b * 4 + 2 * t + 2)
                    sp.dma_start(out[bass.ds(b, 1), :, t * HALF:(t + 1) * HALF].rearrange("a p n -> p (a n)"),
                                 out_s[:, t, :]).then_inc(s_out, 16)
            sp.wait_ge(s_out, ONE + 16 * 2 * BATCH)

        @block.tensor
        def _(pe):
            mm = nc.tensor.matmul

            def ln_mean(n, src, t, written):
                cols = slice(t * HALF, (t + 1) * HALF)
                if written is not None:
                    pe.wait_ge(s_lin, written + 1)
                mm(acc[:, cols], mean_w[:], src[:, cols], start=True, stop=True).then_inc(s_lmean, 1)

            def ln_variance(n, t):
                cols = slice(t * HALF, (t + 1) * HALF)
                pe.wait_ge(s_lsq, n + 1)
                mm(red[:, cols], mean_w[:], h_sq[:, cols], start=True, stop=True).then_inc(s_lvar, 1)

            def layer_norm(n, src, written=None):
                for t in range(2):
                    ln_mean(n + t, src, t, None if written is None else written + t)
                for t in range(2):
                    ln_variance(n + t, t)

            pe.wait_ge(s_modw, 48)
            pe.wait_ge(s_silu, 1)
            for m in range(6):
                last = mm(acc[:, m * BATCH:(m + 1) * BATCH], s_wmod[:, m, :], s_sig, start=True, stop=True)
            last.then_inc(s_modp, 1)
            pe.wait_ge(s_const, 16 * 7)
            pe.wait_ge(s_modv, 1)
            with pe.Fori(0, BATCH) as b:
                pe.wait_ge(s_x, b * 16 + 16)
                layer_norm(b * 2, h_in)

            with pe.Fori(0, LAYERS) as l:
                with pe.Fori(0, BATCH) as b:
                    it = l * BATCH + b

                    def take(u):
                        pe.wait_ge(s_free, ONE + it * RING + u - 1) if u else pe.wait_ge(s_free, ONE + it * RING)
                        return ring[:, u % 2, :]

                    pe.wait_ge(s_wa, it * 16 + 16)
                    pe.wait_ge(s_h, it * 16 + 16)
                    for t in range(2):
                        dst = take(K_U[t])
                        mm(dst[:, 0:HALF], wa_s[:, D:2 * D], h_in[:, t * HALF:(t + 1) * HALF],
                           start=True, stop=True).then_inc(s_full, 1)
                    for u, w in ((Q_U[0], 0), (V_U[0], 2)):
                        dst = take(u)
                        for t in range(2):
                            last = mm(dst[:, t * HALF:(t + 1) * HALF], wa_s[:, w * D:(w + 1) * D],
                                      h_in[:, t * HALF:(t + 1) * HALF], start=True, stop=True)
                        last.then_inc(s_full, 1)
                    pe.wait_ge(s_kx, it * 256 + 256)
                    pe.wait_ge(s_free, ONE + it * RING + Q_U[0] + 1)
                    for u in range(SUNITS):
                        dst = take(S_U + u)
                        for j, col, nj in in_unit(u):
                            if j == BLOCKS // 2:
                                last.then_inc(s_sdone, 1)
                            jh, jr = divmod(j, BLOCKS // 2)
                            keys = diag[:, jh, :, jr]
                            for top in ((0, 1) if nj > HALF else (None,)):
                                for off, n, rs in pieces(j, nj, fixed_top=top):
                                    c = col - u * UNIT + off
                                    last = mm(view_block(dst[:, c:c + n], rs), keys, view_queries(q_t[:], rs),
                                              start=True, stop=True)
                            if (j, col, nj) == in_unit(u)[-1]:
                                last.then_inc(s_full, 1)
                    pe.wait_ge(s_max, it * (NMAX + 1) + NMAX + 1)
                    for c in range(8):
                        last = nc.tensor.transpose(acc[:, c * 128:(c + 1) * 128], den[:, c * 128:(c + 1) * 128],
                                                   ident[:])
                    last.then_inc(s_rtr, 1)
                    pe.wait_ge(s_m, it * 3 + 3)
                    for c in range(8):
                        last = nc.tensor.transpose(red[:, c * 128:(c + 1) * 128], den[:, c * 128:(c + 1) * 128],
                                                   ident[:])
                    last.then_inc(s_mb, 1)
                    pe.wait_ge(s_vx0, it * 256 + 256)
                    for u in range(SUNITS):
                        pe.wait_ge(s_exp, it * SUNITS + u + 1)
                        for j, col, nj in in_unit(u):
                            if j == BLOCKS // 2:
                                pe.wait_ge(s_vx1, it * 256 + 256)
                            jh, jr = divmod(j, BLOCKS // 2)
                            vals = diag[:, 2 if jh == 0 else 0, :, jr]
                            for top in (0, 1):
                                for off, n, rs in pieces(j, nj, fixed_top=top):
                                    last = mm(view_queries(acc[:], rs), vals,
                                              view_block(score[:, col + off:col + off + n], rs),
                                              start=(j == 0), stop=(j == BLOCKS - 1 or (j == BLOCKS // 2 - 1 and top == 1)),
                                              skip_group_check=True)
                    last.then_inc(s_pv, 1)
                    pe.wait_ge(s_den, it * NMAX + NMAX)
                    pe.wait_ge(s_shift, it * SUNITS + SUNITS)
                    for t in range(2):
                        last = mm(red[:, t * HALF:(t + 1) * HALF], ones_b[:], den[:, t * HALF:(t + 1) * HALF],
                                  start=True, stop=True)
                    last.then_inc(s_denb, 1)
                    pe.wait_ge(s_wb, it * 16 + 16)
                    pe.wait_ge(s_fin, it * 4 + 4)
                    for t in range(2):
                        mm(red[:, t * HALF:(t + 1) * HALF], wo, q_t[:, t * HALF:(t + 1) * HALF],
                           start=True, stop=True).then_inc(s_op, 1)
                    layer_norm(it * ITER_LN + PRE_LN, k_t, it * ITER_LN)
                    for t in range(2):
                        pe.wait_ge(s_lout, ONE + it * ITER_LN + PRE_LN + t + 1)
                        for p in range(2):
                            dst = take(G_U + 2 * t + p)
                            for c in range(2):
                                last = mm(dst[:, c * HALF:(c + 1) * HALF], w1[:, 2 * p + c, :],
                                          q_t[:, t * HALF:(t + 1) * HALF], start=True, stop=True)
                            last.then_inc(s_full, 1)
                    for t in range(2):
                        pe.wait_ge(s_free, ONE + it * RING + G_U + 2 * t + 2)
                        for c in range(FCH):
                            last = mm(acc[:, t * HALF:(t + 1) * HALF], w2[:, c, :], gl[:, t, c, :],
                                      start=(c == 0), stop=(c == FCH - 1))
                        last.then_inc(s_w2, 1)
                    layer_norm(it * ITER_LN + PRE_LN + 2, k_t, it * ITER_LN + 2)

            base = PRE_LN + ITERS * ITER_LN
            with pe.Fori(0, BATCH) as b:
                pe.wait_ge(s_h, (ITERS + 1) * 16 + b * 16)
                layer_norm(base + b * 4, h_in)
                layer_norm(base + b * 4 + 2, k_t, ITERS * ITER_LN + b * 2)
            pe.wait_ge(s_modw, 48 + 96)
            pe.wait_ge(s_lout, ONE + base + 4 * BATCH)
            for c in range(TILES):
                last = mm(acc[:, c * EXPERTS:(c + 1) * EXPERTS], hm[:, c * 128:(c + 1) * 128], e_wg,
                          start=True, stop=True)
            last.then_inc(s_gate, 1)
            pe.wait_ge(s_gv, GATE_STEPS)
            for r in range(4):
                if r >= 2:
                    pe.wait_ge(s_ctc, r - 1)
                for c in range(8):
                    k = r * 8 + c
                    last = nc.tensor.transpose(ring[0:EXPERTS, r % 2, c * 128:(c + 1) * 128],
                                               m_a[:, k * EXPERTS:(k + 1) * EXPERTS], ident[:])
                last.then_inc(s_ctp, 1)
            pe.wait_ge(s_ctc, 4)
            with pe.Fori(0, BATCH) as b:
                for t in range(2):
                    for c in range(MCH + 1):
                        if c < MCH:
                            n = 2 * MCH * b + t * MCH + c
                            q = (t * MCH + c) % 2
                            rhs = hm[:, bass.ds(b * SEQ + t * HALF, HALF)]
                            pe.wait_ge(s_act, ONE + (n - 1 if t or c else n))
                            mm(ring[:, q, 0:HALF], e_w1[:, c, :], rhs, start=True, stop=True)
                            mm(ring[:, q, HALF:UNIT], e_w3[:, c, :], rhs, start=True, stop=True).then_inc(s_gu, 1)
                            if c < MCH - 1:
                                mm(red[:, q * HALF:(q + 1) * HALF], e_ind[:, c, :],
                                   comb_t[:, bass.ds(b * SEQ + t * HALF, HALF)], start=True, stop=True)\
                                    .then_inc(s_cb, 1)
                        if c >= 1:
                            n = 2 * MCH * b + t * MCH + c - 1
                            pe.wait_ge(s_act, ONE + n + 1)
                            if c == 1:
                                pe.wait_ge(s_od, ONE + b * 4)
                            last = mm(acc[:, t * HALF:(t + 1) * HALF], e_w2[:, c - 1, :],
                                      m_z[:, (t * MCH + c - 1) % 2, :], start=(c == 1), stop=(c == MCH))
                    last.then_inc(s_eo, 1)

        @block.scalar
        def _(act):
            A = nc.scalar.activation

            def ln_square(n, t):
                cols = slice(t * HALF, (t + 1) * HALF)
                act.wait_ge(s_lcen, n + 1)
                A(h_sq[:, cols], k_t[:, cols], ACT.Square).then_inc(s_lsq, 1)

            def ln_rstd(n, t):
                cols = slice(t * HALF, (t + 1) * HALF)
                act.wait_ge(s_lvar, n + 1)
                A(red[:, cols], red[:, cols], ACT.Ln, bias=eps[:]).then_inc(s_lln, 1)
                act.wait_ge(s_lln, n + 1)
                A(red[:, cols], red[:, cols], ACT.Exp, scale=-0.5).then_inc(s_lstd, 1)

            def ln_affine(n, t, dst, g, beta):
                cols = slice(t * HALF, (t + 1) * HALF)
                act.wait_ge(s_lnorm, n + 1)
                A(dst[:, cols] if not isinstance(dst, list) else dst[t], h_sq[:, cols], ACT.Identity,
                  scale=g, bias=beta).then_inc(s_lout, 1)

            def layer_norm(n, dst, g, beta):
                for t in range(2):
                    ln_square(n + t, t)
                for t in range(2):
                    ln_rstd(n + t, t)
                for t in range(2):
                    ln_affine(n + t, t, dst, g, beta)

            act.wait_ge(s_modw, 48)
            A(s_sgn[:, 0:BATCH], s_c, ACT.Exp, scale=-1.0).then_inc(s_silu_e, 1)
            act.wait_ge(s_modv, MOD_STEPS)
            act.wait_ge(s_eps, 2)
            act.wait_ge(s_const, 16 * 7)
            with act.Fori(0, BATCH) as b:
                act.wait_ge(s_lout, ONE + b * 2)
                A(cur[:], mod[:, :, bass.ds(b, 1)].rearrange("p m a -> p (m a)"), ACT.Copy).then_inc(s_cur, 1)
                act.wait_ge(s_cur, b + 1)
                act.wait_ge(s_pe, ONE + b * 2)
                act.wait_ge(s_hst, ONE + b * 16)
                layer_norm(b * 2, q_t, cur[:, 1:2], cur[:, 0:1])

            with act.Fori(0, LAYERS) as l:
                with act.Fori(0, BATCH) as b:
                    it = l * BATCH + b
                    act.wait_ge(s_wa, it * 16 + 16)
                    act.wait_ge(s_hst, ONE + it * 16 + 64)
                    for t in range(2):
                        act.wait_ge(s_full, it * RING + K_U[t] + 1)
                        A(k_t[:, t * HALF:(t + 1) * HALF].rearrange("p (l j) -> p j l", l=LO),
                          ring[:, K_U[t] % 2, 0:HALF].rearrange("p (j l) -> p j l", l=LO), ACT.Identity, bias=bk)\
                            .then_inc(s_free, 1)
                    act.wait_ge(s_full, it * RING + Q_U[0] + 1)
                    A(q_t[:], ring[:, Q_U[0] % 2, :], ACT.Identity, bias=bq).then_inc(s_free, 1)
                    act.wait_ge(s_full, it * RING + V_U[0] + 1)
                    A(n_t.rearrange("p (l j) -> p j l", l=LO),
                      ring[:, V_U[0] % 2, :].rearrange("p (j l) -> p j l", l=LO), ACT.Identity, bias=bv)\
                        .then_inc(s_free, 1)
                    for u in range(SUNITS):
                        act.wait_ge(s_full, it * RING + S_U + u + 1)
                        for a, z in unit_spans(u):
                            last = A(score[:, u * UNIT + a:u * UNIT + z], ring[:, (S_U + u) % 2, a:z], ACT.Copy,
                                     scale=SCALE)
                        last.then_inc(s_free, 1)
                    act.wait_ge(s_mb, it + 1)
                    A(e0, red[:], ACT.Exp, scale=-1.0).then_inc(s_e0, 1)
                    for u in range(SUNITS):
                        act.wait_ge(s_shift, it * SUNITS + u + 1)
                        for a, z in unit_spans(u):
                            last = A(score[:, u * UNIT + a:u * UNIT + z], score[:, u * UNIT + a:u * UNIT + z], ACT.Exp)
                        last.then_inc(s_exp, 1)
                    layer_norm(it * ITER_LN + PRE_LN, q_t, g1, be1)
                    act.wait_ge(s_lout, ONE + it * ITER_LN + PRE_LN + 2)
                    for t in range(2):
                        for p in range(2):
                            u = G_U + 2 * t + p
                            act.wait_ge(s_full, it * RING + u + 1)
                            for c in range(2):
                                last = A(gl[:, t, 2 * p + c, :], ring[:, u % 2, c * HALF:(c + 1) * HALF], ACT.Gelu,
                                         bias=b1[2 * p + c])
                            last.then_inc(s_free, 1)
                    layer_norm(it * ITER_LN + PRE_LN + 2, q_t, g2, be2)
                    act.wait_ge(s_lout, ONE + it * ITER_LN + PRE_LN + ITER_LN)
                    act.dma_start(h_dram[bass.ds(b, 1)].rearrange("a p n -> p (a n)"), q_t[:]).then_inc(s_hst, 16)

            base = PRE_LN + ITERS * ITER_LN
            with act.Fori(0, BATCH) as b:
                act.wait_ge(s_lout, ONE + base + b * 4)
                act.wait_ge(s_x2, ONE + b * 2)
                A(cur[:], mod[:, :, bass.ds(b, 1)].rearrange("p m a -> p (m a)"), ACT.Copy).then_inc(s_cur, 1)
                act.wait_ge(s_cur, BATCH + b + 1)
                layer_norm(base + b * 4, q_t, lnf_s[:, 0:1], lnf_s[:, 1:2])
                layer_norm(base + b * 4 + 2, [hm[:, bass.ds(b * SEQ + t * HALF, HALF)] for t in range(2)],
                           cur[:, 4:5], cur[:, 3:4])
            act.wait_ge(s_gate, 1)
            A(m_a, acc[:, 0:512], ACT.Exp, scale=-1.0).then_inc(s_gexp, 1)
            for r in range(4):
                act.wait_ge(s_ctp, r + 1)
                A(comb_t[:, r * SEQ:(r + 1) * SEQ], ring[0:EXPERTS, r % 2, :], ACT.Copy).then_inc(s_ctc, 1)
            with act.Fori(0, BATCH) as b:
                act.wait_ge(s_od, ONE + b * 4)
                A(cur[:], mod[:, :, bass.ds(b, 1)].rearrange("p m a -> p (m a)"), ACT.Copy).then_inc(s_cur, 1)
                for t in range(2):
                    for c in range(MCH):
                        n = 2 * MCH * b + t * MCH + c
                        q = (t * MCH + c) % 2
                        act.wait_ge(s_gu, n + 1)
                        act.wait_ge(s_act, ONE + (n - 1 if t or c else n))
                        A(m_sg[:, q, :], ring[:, q, 0:HALF], ACT.Silu).then_inc(s_sg, 1)

        @block.vector
        def _(dve):
            V = nc.vector

            def ln_centre(n, src, t):
                cols = slice(t * HALF, (t + 1) * HALF)
                dve.wait_ge(s_lmean, n + 1)
                V.tensor_tensor(k_t[:, cols], src[:, cols], acc[:, cols], ALU.subtract).then_inc(s_lcen, 1)

            def ln_norm(n, t):
                cols = slice(t * HALF, (t + 1) * HALF)
                dve.wait_ge(s_lstd, n + 1)
                V.tensor_tensor(h_sq[:, cols], red[:, cols], k_t[:, cols], ALU.mult).then_inc(s_lnorm, 1)

            def layer_norm(n, src):
                for t in range(2):
                    ln_centre(n + t, src, t)
                for t in range(2):
                    ln_norm(n + t, t)

            for a in range(3):
                V.memset(diag[:, a, :, :], 0.0).then_inc(s_zero, 1)
            V.memset(eps[:], EPS).then_inc(s_eps, 1)
            V.memset(one[:], 1.0).then_inc(s_eps, 1)
            mv = chain(dve, s_dv)
            dve.wait_ge(s_silu_e, 1)
            mv(V.tensor_scalar(s_sgn[:, 0:BATCH], s_sgn[:, 0:BATCH], 1.0, None, ALU.add))
            mv(V.reciprocal(s_sgn[:, 0:BATCH], s_sgn[:, 0:BATCH]))
            V.tensor_tensor(s_sig, s_c, s_sgn[:, 0:BATCH], ALU.mult).then_inc(s_silu, 1)
            dve.wait_ge(s_modp, 1)
            V.tensor_copy(mod[:], acc[:, 0:6 * BATCH].rearrange("p (m b) -> p m b", m=6)).then_inc(s_modv, 1)
            dve.wait_ge(s_modv, 1)
            dve.wait_ge(s_silu, 1)
            for m in (1, 4):
                V.tensor_scalar(mod[:, m, :], mod[:, m, :], 1.0, None, ALU.add).then_inc(s_modv, 1)
            for m in (2, 5):
                mv(V.tensor_scalar(s_sgn[:, 0:BATCH], mod[:, m, :], 0.0, 2.0, ALU.is_ge, ALU.mult))
                mv(V.tensor_scalar(s_sgn[:, BATCH:2 * BATCH], mod[:, m, :], -1.0, 0.25, ALU.mult, ALU.max))
                mv(V.tensor_tensor(s_sgn[:, BATCH:2 * BATCH], s_sgn[:, BATCH:2 * BATCH], mod[:, m, :], ALU.max))
                mv(V.tensor_scalar(s_sgn[:, 0:BATCH], s_sgn[:, 0:BATCH], -1.0, None, ALU.add))
                mv(V.tensor_tensor(mod[:, m, :], s_sgn[:, 0:BATCH], s_sgn[:, BATCH:2 * BATCH], ALU.mult)) \
                    if m == 2 else V.tensor_tensor(mod[:, m, :], s_sgn[:, 0:BATCH], s_sgn[:, BATCH:2 * BATCH],
                                                   ALU.mult).then_inc(s_modv, 1)
            assert MOD_STEPS == 4
            dve.wait_ge(s_modw, 48)
            with dve.Fori(0, BATCH) as b:
                dve.wait_ge(s_x, b * 16 + 16)
                layer_norm(b * 2, h_in)
                for t in range(2):
                    cols = slice(t * HALF, (t + 1) * HALF)
                    dve.wait_ge(s_lout, ONE + b * 2 + t + 1)
                    V.tensor_tensor(q_t[:, cols], q_t[:, cols], s_pe_view[:, cols], ALU.add).then_inc(s_pe, 1)

            with dve.Fori(0, LAYERS) as l:
                with dve.Fori(0, BATCH) as b:
                    it = l * BATCH + b
                    base = it * (NMAX + 1)
                    for k, (u, col, off, n, rs) in enumerate(MAXP):
                        if k == 0 or MAXP[k - 1][0] != u:
                            dve.wait_ge(s_free, ONE + it * RING + S_U + u + 1)
                        if k:
                            dve.wait_ge(s_max, base + k)
                        s = view_block(score[:, col + off:col + off + n], rs)
                        r = view_queries(red[:], rs)
                        if k == 0:
                            V.tensor_copy(r, s).then_inc(s_max, 1)
                        else:
                            V.tensor_tensor(r, r, s, ALU.max).then_inc(s_max, 1)
                    dve.wait_ge(s_max, base + NMAX)
                    neg_b = neg[:].unsqueeze(1).broadcast_to([128, BLOCKS, LO])
                    V.tensor_tensor(den.rearrange("p (i l) -> p i l", l=LO),
                                    red[:].rearrange("p (i l) -> p i l", l=LO), neg_b, ALU.add).then_inc(s_max, 1)
                    dve.wait_ge(s_rtr, it + 1)
                    V.tensor_reduce(m_tok[:], acc[:].rearrange("p (g l) -> p g l", l=LO), AX_X, ALU.max)\
                        .then_inc(s_m, 1)
                    dve.wait_ge(s_m, it * 3 + 1)
                    V.tensor_scalar(den[:, 0:128].rearrange("p (h l) -> p h l", l=LO),
                                    m_tok[:, 0:HEADS].unsqueeze(2).broadcast_to([128, HEADS, LO]),
                                    floor[:], None, ALU.max).then_inc(s_m, 1)
                    V.tensor_scalar(den[:, 128:].rearrange("p (h l) -> p h l", l=LO),
                                    m_tok[:, HEADS:].unsqueeze(2).broadcast_to([128, BLOCKS - HEADS, LO]),
                                    0.0, None, ALU.max).then_inc(s_m, 1)
                    dve.wait_ge(s_e0, it + 1)
                    red_v = red[:].rearrange("p (i l) -> p i l", l=LO)
                    V.scalar_tensor_tensor(out=red_v, in0=red_v, scalar=-1.0, in1=neg_b, op0=ALU.mult, op1=ALU.add)\
                        .then_inc(s_b, 1)
                    dve.wait_ge(s_b, it + 1)
                    for k, (u, col, off, n, rs) in enumerate(MAXP):
                        s = view_block(score[:, col + off:col + off + n], rs)
                        last = V.tensor_tensor(s, view_queries(red[:], rs), s, ALU.add)
                        if k == NMAX - 1 or MAXP[k + 1][0] != u:
                            last.then_inc(s_shift, 1)
                    f = it * 4
                    dve.wait_ge(s_denb, it + 1)
                    dve.wait_ge(s_ec, it * 2 + 2)
                    V.tensor_tensor(den, red[:], e0, ALU.add).then_inc(s_fin, 1)
                    dve.wait_ge(s_fin, f + 1)
                    V.reciprocal(den, den).then_inc(s_fin, 1)
                    dve.wait_ge(s_pv, ONE + it + 1)
                    V.tensor_tensor(acc[:], acc[:], n_t, ALU.add).then_inc(s_fin, 1)
                    dve.wait_ge(s_fin, f + 3)
                    V.tensor_tensor(q_t[:], acc[:], den, ALU.mult).then_inc(s_fin, 1)
                    for t in range(2):
                        cols = slice(t * HALF, (t + 1) * HALF)
                        dve.wait_ge(s_op, it * 2 + t + 1)
                        dve.wait_ge(s_kx, it * 256 + 256)
                        V.scalar_tensor_tensor(out=k_t[:, cols], in0=red[:, cols], scalar=bo, in1=h_in[:, cols],
                                               op0=ALU.add, op1=ALU.add).then_inc(s_lin, 1)
                    layer_norm(it * ITER_LN + PRE_LN, k_t)
                    for t in range(2):
                        cols = slice(t * HALF, (t + 1) * HALF)
                        dve.wait_ge(s_w2, it * 2 + t + 1)
                        V.scalar_tensor_tensor(out=k_t[:, cols], in0=acc[:, cols], scalar=b2, in1=q_t[:, cols],
                                               op0=ALU.add, op1=ALU.add).then_inc(s_lin, 1)
                    layer_norm(it * ITER_LN + PRE_LN + 2, k_t)

            base = PRE_LN + ITERS * ITER_LN
            with dve.Fori(0, BATCH) as b:
                dve.wait_ge(s_h, (ITERS + 1) * 16 + b * 16)
                dve.wait_ge(s_lnorm, base + b * 4)
                layer_norm(base + b * 4, h_in)
                dve.wait_ge(s_x, (BATCH + 1) * 16 + b * 16)
                dve.wait_ge(s_cur, BATCH + b + 1)
                for t in range(2):
                    cols = slice(t * HALF, (t + 1) * HALF)
                    dve.wait_ge(s_lout, ONE + base + b * 4 + t + 1)
                    V.scalar_tensor_tensor(out=k_t[:, cols], in0=q_t[:, cols], scalar=cur[:, 2:3],
                                           in1=x2[:, bass.ds(b * SEQ + t * HALF, HALF)], op0=ALU.mult,
                                           op1=ALU.add).then_inc(s_x2, 1)
                    dve.wait_ge(s_x2, ONE + b * 2 + t + 1)
                    V.tensor_scalar(x2[:, bass.ds(b * SEQ + t * HALF, HALF)], k_t[:, cols], 1.0, None, ALU.mult)\
                        .then_inc(s_lin, 1)
                layer_norm(base + b * 4 + 2, k_t)

            g = chain(dve, s_dv, start=mv.count[0])
            dve.wait_ge(s_gexp, 1)
            dve.wait_ge(s_modw, 48 + 96)
            g(V.tensor_scalar(m_g, m_a, 1.0, None, ALU.add))
            g(V.reciprocal(m_g, m_g))
            s4 = m_g.rearrange("p (q e) -> p q e", e=4)
            hi1, lo1, hi2, lo2 = m_t
            g(V.tensor_tensor(hi1, s4[:, :, 0], s4[:, :, 1], ALU.max))
            g(V.tensor_tensor(lo1, s4[:, :, 0], s4[:, :, 1], ALU.min))
            g(V.tensor_tensor(hi2, s4[:, :, 2], s4[:, :, 3], ALU.max))
            g(V.tensor_tensor(lo2, s4[:, :, 2], s4[:, :, 3], ALU.min))
            g(V.tensor_tensor(m_gs, hi1, hi2, ALU.max))
            g(V.tensor_tensor(hi1, hi1, hi2, ALU.min))
            g(V.tensor_tensor(lo1, lo1, lo2, ALU.max))
            g(V.tensor_tensor(hi1, hi1, lo1, ALU.max))
            g(V.tensor_tensor(m_gs, m_gs, hi1, ALU.add))

            def ranks(dst, val, width):
                n = TILES * width * width
                v = val.rearrange("p (t e) -> p t e", e=width)
                other = v.unsqueeze(2).broadcast_to([128, TILES, width, width])
                own = v.unsqueeze(3).broadcast_to([128, TILES, width, width])
                c1 = m_c1[:, 0:n].rearrange("p (t e o) -> p t e o", t=TILES, e=width)
                c2 = m_c2[:, 0:n].rearrange("p (t e o) -> p t e o", t=TILES, e=width)
                tri = e_tri[:, 0:width, 0:width].unsqueeze(1).broadcast_to([128, TILES, width, width])
                g(V.tensor_tensor(c1, other, own, ALU.is_equal))
                g(V.tensor_tensor(c1, c1, tri, ALU.mult))
                g(V.tensor_tensor(c2, other, own, ALU.is_gt))
                g(V.tensor_tensor(c1, c1, c2, ALU.add))
                g(V.tensor_reduce(dst, m_c1[:, 0:n].rearrange("p (q o) -> p q o", o=width), AX_X, ALU.add))

            ranks(m_al, m_gs, GROUPS)
            g(V.tensor_scalar(m_al, m_al, 1.5, None, ALU.is_lt))
            al = m_al.unsqueeze(2).broadcast_to([128, TILES * GROUPS, 4])
            m_b4 = m_b.rearrange("p (q e) -> p q e", e=4)
            g(V.tensor_tensor(m_b4, s4, al, ALU.mult))
            g(V.tensor_scalar(m_al, m_al, -1.0, None, ALU.add))
            g(V.tensor_tensor(m_b4, m_b4, al, ALU.add))
            ranks(m_a, m_b, EXPERTS)
            g(V.tensor_scalar(m_a, m_a, 3.5, None, ALU.is_lt))
            g(V.tensor_tensor(m_a, m_a, m_g, ALU.mult))
            a3 = m_a.rearrange("p (t e) -> p t e", e=EXPERTS)
            g(V.tensor_reduce(m_t[0][:, 0:TILES], a3, AX_X, ALU.add))
            g(V.tensor_scalar(m_t[0][:, 0:TILES], m_t[0][:, 0:TILES], 1e-6, None, ALU.add))
            g(V.reciprocal(m_t[0][:, 0:TILES], m_t[0][:, 0:TILES]))
            V.tensor_tensor(a3, a3, m_t[0][:, 0:TILES].unsqueeze(2).broadcast_to([128, TILES, EXPERTS]), ALU.mult)\
                .then_inc(s_gv, GATE_STEPS)
            with dve.Fori(0, BATCH) as b:
                dve.wait_ge(s_cur, 2 * BATCH + b + 1)
                for t in range(2):
                    for c in range(MCH):
                        n = 2 * MCH * b + t * MCH + c
                        q = (t * MCH + c) % 2
                        dve.wait_ge(s_sg, n + 1)
                        if c < MCH - 1:
                            V.tensor_tensor(m_y[:, q, :], m_sg[:, q, :], ring[:, q, HALF:UNIT], ALU.mult)\
                                .then_inc(s_hvs, 1)
                            steps = 2 * (MCH - 1) * b + t * (MCH - 1) + c + 1
                            dve.wait_ge(s_hvs, steps)
                            dve.wait_ge(s_cb, steps)
                            V.tensor_tensor(m_z[:, q, :], m_y[:, q, :], red[:, q * HALF:(q + 1) * HALF], ALU.mult)\
                                .then_inc(s_act, 1)
                        else:
                            V.tensor_tensor(m_z[:, q, :], m_sg[:, q, :], ring[:, q, HALF:UNIT], ALU.mult)\
                                .then_inc(s_act, 1)
                    cols = slice(t * HALF, (t + 1) * HALF)
                    dve.wait_ge(s_eo, b * 2 + t + 1)
                    dve.wait_ge(s_out, ONE + b * 32)
                    V.tensor_scalar(out_s[:, t, :], acc[:, cols], cur[:, 5:6], None, ALU.mult).then_inc(s_od, 1)
                    dve.wait_ge(s_od, ONE + b * 4 + 2 * t + 1)
                    V.tensor_tensor(out_s[:, t, :], out_s[:, t, :], x2[:, bass.ds(b * SEQ + t * HALF, HALF)],
                                    ALU.add).then_inc(s_od, 1)

        @block.gpsimd
        def _(pool):
            P = nc.gpsimd
            pool.wait_ge(s_eps, 2)
            pool.wait_ge(s_const, 16 * 7)
            with pool.Fori(0, LAYERS) as l:
                with pool.Fori(0, BATCH) as b:
                    it = l * BATCH + b
                    zb = it * 11
                    pool.wait_ge(s_vst, ONE + it * 16 + 16)
                    for k in range(10):
                        v = n_t.rearrange("p (a s w) -> p a s w", s=2, w=1 << k)
                        if k:
                            pool.wait_ge(s_z, zb + k)
                        P.tensor_tensor(v[:, :, 1, :], v[:, :, 1, :], v[:, :, 0, :], ALU.add).then_inc(s_z, 1)
                    pool.wait_ge(s_z, zb + 10)
                    P.tensor_tensor(n_rev.rearrange("p (j l) -> p j l", l=LO),
                                    n_t[:, SEQ - 1:SEQ].unsqueeze(2).broadcast_to([128, BLOCKS, LO]),
                                    n_t.rearrange("p (l j) -> p j l", l=LO)[:, ::-1, ::-1], ALU.subtract)\
                        .then_inc(s_z, 1)
                    base = it * NMAX
                    pool.wait_ge(s_mb, it + 1)
                    for k, (u, col, off, n, rs) in enumerate(MAXP):
                        if k == 0 or MAXP[k - 1][0] != u:
                            pool.wait_ge(s_exp, it * SUNITS + u + 1)
                        if k:
                            pool.wait_ge(s_den, base + k)
                        s = view_block(score[:, col + off:col + off + n], rs)
                        r = view_queries(den, rs)
                        if k == 0:
                            P.tensor_tensor(r, s, one[:].broadcast_to([128, n]), ALU.mult).then_inc(s_den, 1)
                        else:
                            P.tensor_tensor(r, r, s, ALU.add).then_inc(s_den, 1)
                        if k == 0:
                            pool.wait_ge(s_z, zb + 11)
                            pool.wait_ge(s_e0, it + 1)
                            P.tensor_tensor(n_t, n_rev, e0, ALU.mult).then_inc(s_ec, 1)
                            pool.wait_ge(s_ec, it * 2 + 1)
                            P.tensor_tensor(e0, e0, cnt[:], ALU.mult).then_inc(s_ec, 1)



def _constants():
    import numpy as np
    pos = np.arange(SEQ)
    level = np.frexp((pos + 1).astype(np.float64))[1] - 1
    coord = (pos >> level) / 2.0 ** level
    div = np.exp(np.arange(0, D, 2, dtype=np.float64) * -(np.log(10000.0) / D))
    ang = pos[:, None].astype(np.float64) * div[None, :]
    pe = np.zeros((SEQ, D), np.float32)
    pe[:, 0::2] = (np.sin(ang) * coord[:, None]).astype(np.float32)
    pe[:, 1::2] = (np.cos(ang) * coord[:, None]).astype(np.float32)
    p = np.arange(128)
    lo = np.arange(LO)
    queries = np.arange(SEQ)
    allowed = np.array([1 << (10 - bin(int(i)).count("1")) for i in queries])
    floor = np.zeros((128, 1), np.float32)
    floor[0] = -3e38
    expert = np.arange(EXPERTS)
    chunk = np.arange(MCH - 1)
    ind = expert[:, None, None] == 2 * chunk[None, :, None] + (p // EF)[None, None, :]
    return {
        "pe_t": np.ascontiguousarray(pe.T),
        "ident": np.eye(128, dtype=np.float32),
        "ones": (p[:, None] // HD == p[None, :] // HD).astype(np.float32),
        "mean": np.full((128, 128), 1.0 / D, np.float32),
        "neg": np.where((p[:, None] % LO) & lo[None, :], np.float32(NEG), np.float32(0)).astype(np.float32),
        "cnt": np.broadcast_to((SEQ - allowed).astype(np.float32), (128, SEQ)).copy(),
        "floor": floor,
        "tri": np.broadcast_to((expert[None, :] < expert[:, None]).astype(np.float32), (128, 16, 16)).copy(),
        "ind": ind.astype(np.float32),
    }


def kernel(**inputs):
    import numpy as np
    import concourse.bacc as bacc
    from concourse.bass_utils import run_bass_kernel_spmd

    a = {k: np.asarray(v) for k, v in inputs.items()}
    at = {k[8:]: v for k, v in a.items() if k.startswith("L0_attn_")}
    ff = {k[7:]: v for k, v in a.items() if k.startswith("L0_ffn_")}
    col = lambda v: v.reshape(LAYERS, D, 1)
    const = _constants()
    arrays = {
        "x_t": at["x"].transpose(0, 2, 1),
        "pe_t": const["pe_t"],
        "wa": np.concatenate([at["Wq"], at["Wk"], at["Wv"], col(at["bq"]), col(at["bk"]), col(at["bv"])], axis=2),
        "wb": np.concatenate(
            [at["Wo"], at["W1"], at["W2"].reshape(LAYERS, FCH, D, D).transpose(0, 2, 1, 3).reshape(LAYERS, D, HID)]
            + [col(at[k]) for k in ("bo", "b2", "ln1_g", "ln1_b", "ln2_g", "ln2_b")]
            + [at["b1"].reshape(LAYERS, FCH, D).transpose(0, 2, 1)], axis=2),
        "lnf": np.stack([at["lnf_g"], at["lnf_b"]], axis=1),
        "c_t": a["L0_c"].T,
        "wmod": a["L0_wmod"],
        "w_gate": ff["w_gate"].T,
        "we1": np.concatenate([ff["w1_e"].reshape(EXPERTS * EF, D), ff["w1_s"]]).T.reshape(D, MCH, 128),
        "we3": np.concatenate([ff["w3_e"].reshape(EXPERTS * EF, D), ff["w3_s"]]).T.reshape(D, MCH, 128),
        "we2": np.concatenate([ff["w2_e"].transpose(0, 2, 1).reshape(EXPERTS * EF, D), ff["w2_s"].T])
        .reshape(MCH, 128, D).transpose(1, 0, 2),
        "ident": const["ident"], "ones": const["ones"], "mean": const["mean"], "neg": const["neg"],
        "cnt": const["cnt"], "floor": const["floor"], "tri": const["tri"], "ind": const["ind"],
    }
    nc = bacc.Bacc("TRN2", target_bir_lowering=False, num_devices=1)
    feed, args = {}, []
    for name, v in arrays.items():
        feed[f"in_{name}"] = np.ascontiguousarray(v)
        args.append(nc.dram_tensor(f"in_{name}", v.shape, F32, kind="ExternalInput").ap())
    h_dram = nc.dram_tensor("h_scratch", (BATCH, D, SEQ), F32, kind="Internal").ap()
    v_dram = nc.dram_tensor("v_scratch", (D, SEQ), F32, kind="Internal").ap()
    out = nc.dram_tensor("out_t", (BATCH, D, SEQ), F32, kind="ExternalOutput").ap()
    adaln_kernel(nc, *args, h_dram, v_dram, out)
    r = run_bass_kernel_spmd(nc, [feed], core_ids=[0])
    return np.ascontiguousarray(r.results[0]["out_t"].transpose(0, 2, 1))
```

```python
from contextlib import ExitStack

import concourse.bass as bass
from concourse import mybir

F32 = mybir.dt.float32
ALU = mybir.AluOpType
ACT = mybir.ActivationFunctionType
AX_X = mybir.AxisListType.X

LAYERS, BATCH, SEQ, D, HEADS, HID = 6, 4, 1024, 128, 16, 512
HD = D // HEADS
LO = 8
BITS = 7
BLOCKS = SEQ // LO
HALF = SEQ // 2
ITERS = LAYERS * BATCH
FCH = HID // D
EPS = 1e-5
NEG = -1e30
SCALE = float(1.0 / (HD ** 0.5))
EXPERTS, GROUPS, EF = 16, 4, 64
MCH = 9
TILES = BATCH * SEQ // 128


def block_cols(j):
    return LO << (BITS - bin(j).count("1"))


def packing(js):
    total = sum(block_cols(j) for j in js)
    first = max(block_cols(js[0]) // HALF, 1)
    room = [HALF] * (total // HALF) + [total % HALF]
    banks = [[] for _ in room]
    banks[0] = [js[0]]
    for q in range(first):
        room[q] = 0
    for j in sorted(js[1:], key=lambda j: (-block_cols(j), j)):
        q = max(range(len(room)), key=lambda q: (room[q], q))
        banks[q].append(j)
        room[q] -= block_cols(j)
    assert not any(room)
    mixed = sorted((b for b in banks[first:-1] if len(b) > 1), key=len)
    whole = [b for b in banks[first:-1] if len(b) == 1]
    order = []
    while mixed or whole:
        if mixed:
            order.append(mixed.pop())
        if whole:
            order.append(whole.pop())
    return [j for b in banks[:first] + order + banks[-1:] for j in b]


def placement():
    out, col = [], 0
    for js in (range(BLOCKS // 2), range(BLOCKS // 2, BLOCKS)):
        col = (col + HALF - 1) // HALF * HALF
        for j in packing(js):
            out.append((j, col, block_cols(j)))
            col += block_cols(j)
    return out, col


PLACE, SCORE_COLS = placement()
UNIT = 2 * HALF
SUNITS = (SCORE_COLS + UNIT - 1) // UNIT
GAP = (sum(n for j, _, n in PLACE if j < BLOCKS // 2),
       [c for j, c, _ in PLACE if j == BLOCKS // 2][0])


def pieces(j, n, fixed_top=None, max_runs=2):
    held = {}
    if fixed_top is not None:
        if j >> (BITS - 1) & 1:
            if fixed_top:
                return
        held[BITS - 1] = fixed_top

    def runs(held):
        out = []
        for k in range(BITS - 1, -1, -1):
            kind = "fix" if (j >> k & 1 or k in held) else "free"
            val = held.get(k, 0)
            if out and out[-1][0] == kind and kind == "free":
                out[-1][1] += 1
            elif out and out[-1][0] == kind:
                out[-1] = [kind, out[-1][1] + 1, out[-1][2] * 2 + val]
            else:
                out.append([kind, 1, val])
        return out

    def strided(rs):
        free = [r for r in rs if r[0] == "free"]
        return len(free) - (1 if rs[-1][0] == "free" else 0)

    def split(held):
        rs = runs(held)
        if strided(rs) <= max_runs:
            off = 0
            for k, v in held.items():
                if v:
                    below = sum(1 for q in range(k) if not j >> q & 1)
                    off += LO << below
            cols = LO
            for r in rs:
                if r[0] == "free":
                    cols <<= r[1]
            yield off, cols, rs
            return
        top = max(k for k in range(BITS) if not j >> k & 1 and k not in held)
        yield from split({**held, top: 0})
        yield from split({**held, top: 1})

    yield from split(held)


def view_queries(ap, rs):
    names, sizes, index = [], {}, [slice(None)]
    for q, (kind, bits, val) in enumerate(rs):
        names.append(f"r{q}")
        sizes[f"r{q}"] = 1 << bits
        index.append(slice(None) if kind == "free" else val)
    v = ap.rearrange("p (" + " ".join(names) + " l) -> p " + " ".join(names) + " l", l=LO, **sizes)
    return v[tuple(index) + (slice(None),)]


def view_block(ap, rs):
    free = [(f"r{q}", 1 << bits) for q, (kind, bits, _) in enumerate(rs) if kind == "free"]
    names = " ".join(n for n, _ in free)
    return ap.rearrange(f"p ({names} l) -> p {names} l", l=LO, **dict(free))


LAST_LOW = [j for j, _, _ in PLACE if j < BLOCKS // 2][-1]
LAST_HIGH = PLACE[-1][0]


def adaln_kernel(nc, x_t, pe_t, wa, wb, lnf, c_t, wmod, w_gate, we1, we3, we2,
                 ident_c, sel_c, mean_c, neg_c, cnt_c, floor_c, tri_c, ind_c,
                 h_dram, v_dram, out):
    with ExitStack() as ctx:
        def sb(name, shape):
            return ctx.enter_context(nc.sbuf_tensor(name, shape, F32))

        def sem(name):
            return ctx.enter_context(nc.semaphore(name))

        ring = ctx.enter_context(nc.psum_tensor("ring", [128, 2, UNIT], F32))
        acc = ctx.enter_context(nc.psum_tensor("acc", [128, SEQ], F32))
        red = ctx.enter_context(nc.psum_tensor("red", [128, SEQ], F32))

        diag = sb("diag", [128, 3, 128, BLOCKS // 2])
        score = sb("score", [128, SCORE_COLS])
        h_in = sb("h_in", [128, SEQ])
        q_t = sb("q_t", [128, SEQ])
        k_t = sb("k_t", [128, SEQ])
        n_t = sb("n_t", [128, SEQ])
        att = sb("att", [128, SEQ])
        res = sb("res", [128, SEQ])
        gl = sb("gl", [128, FCH, HALF])
        h_sq = gl[:, 0:2, :].rearrange("p t n -> p (t n)")
        wa_s = sb("wa_s", [128, 3 * D + 3])
        wb_s = sb("wb_s", [128, D + 2 * HID + 6 + FCH])
        ident = sb("ident", [128, 128])
        mean_w = sb("mean_w", [128, 128])
        neg = sb("neg", [128, LO])
        cnt = sb("cnt", [128, SEQ // 128])
        sel = sb("sel", [128, HEADS])
        floor = sb("floor", [128, 1])
        m_tok = sb("m_tok", [128, BLOCKS])
        e_tok = sb("e_tok", [128, BLOCKS])
        mod = sb("mod", [128, 6, BATCH])
        cur = sb("cur", [128, 6])
        lnf_s = sb("lnf_s", [128, 2])
        eps = sb("eps", [128, 1])
        one = sb("one", [128, 1])

        bq, bk, bv = (wa_s[:, 3 * D + i:3 * D + i + 1] for i in range(3))
        wo = wb_s[:, 0:D]
        w1 = wb_s[:, D:D + HID].rearrange("p (c n) -> p c n", c=FCH)
        w2 = wb_s[:, D + HID:D + 2 * HID].rearrange("p (c n) -> p c n", c=FCH)
        vec = D + 2 * HID
        bo, b2, g1, be1, g2, be2 = (wb_s[:, vec + i:vec + i + 1] for i in range(6))
        b1 = [wb_s[:, vec + 6 + c:vec + 7 + c] for c in range(FCH)]

        s_wmod = score[:, 0:6 * D].rearrange("p (m n) -> p m n", m=6)
        s_c = score[:, 6 * D:6 * D + BATCH]
        s_sig = score[:, 6 * D + BATCH:6 * D + 2 * BATCH]
        s_sgn = score[:, 6 * D + 2 * BATCH:6 * D + 4 * BATCH]
        s_pe_view = score[:, 2 * UNIT:3 * UNIT]
        hm = score[:, 0:4 * SEQ]
        x2 = score[:, 4 * SEQ:8 * SEQ]
        m_g = score[:, 8 * SEQ:8 * SEQ + 512]
        m_a = score[:, 8 * SEQ + 512:9 * SEQ]
        m_b = score[:, 9 * SEQ:9 * SEQ + 512]
        m_gs = score[:, 9 * SEQ + 512:9 * SEQ + 640]
        m_al = score[:, 9 * SEQ + 640:9 * SEQ + 768]
        m_t = [score[:, 9 * SEQ + 768 + 128 * i:9 * SEQ + 896 + 128 * i] for i in range(4)]
        m_rep = score[:, 10 * SEQ + 512:11 * SEQ]
        comb_t = score[0:EXPERTS, 11 * SEQ:15 * SEQ]
        out_s = score[:, 15 * SEQ:15 * SEQ + 2 * HALF].rearrange("p (a n) -> p a n", a=2)
        m_sg = score[:, 16 * SEQ:17 * SEQ].rearrange("p (a n) -> p a n", a=2)
        dflat = diag[:, :, :, :].rearrange("p a m j -> p (a m j)")
        m_c1 = dflat[:, 0:8192]
        m_c2 = dflat[:, 8192:16384]
        o = 16384
        e_w1 = dflat[:, o:o + MCH * 128].rearrange("p (c n) -> p c n", c=MCH)
        e_w3 = dflat[:, o + 1152:o + 2304].rearrange("p (c n) -> p c n", c=MCH)
        e_w2 = dflat[:, o + 2304:o + 3456].rearrange("p (c n) -> p c n", c=MCH)
        e_wg = dflat[:, o + 3456:o + 3472]
        e_tri = dflat[:, o + 3472:o + 3728].rearrange("p (a b) -> p a b", a=16)
        e_ind = dflat[0:EXPERTS, o + 3728:o + 4752].rearrange("p (c n) -> p c n", c=8)
        m_y = dflat[:, o + 4752:o + 5776].rearrange("p (a n) -> p a n", a=2)
        m_z = dflat[:, o + 5776:o + 6800].rearrange("p (a n) -> p a n", a=2)

        s_const = sem("const_loaded")
        s_zero = sem("diag_zeroed")
        s_eps = sem("eps_written")
        s_modw = sem("mod_weights_loaded")
        s_silu_e = sem("silu_exp_ready")
        s_silu = sem("silu_ready")
        s_dv = sem("vector_chain")
        s_modp = sem("mod_product_ready")
        s_modv = sem("mod_vector_steps")
        s_x = sem("x_loaded")
        s_cur = sem("mod_column_copied")
        s_pe = sem("pos_added")
        s_hst = sem("h_stored")
        s_h = sem("h_loaded")
        s_wa = sem("projection_weights_loaded")
        s_wb = sem("ffn_weights_loaded")
        s_full = sem("ring_unit_filled")
        s_free = sem("ring_unit_drained")
        s_vst = sem("v_stored")
        s_kx = sem("diag_keys_loaded")
        s_vx0 = sem("diag_values_low_loaded")
        s_vx1 = sem("diag_values_high_loaded")
        s_sdone = sem("score_halves_done")
        s_max = sem("max_steps")
        s_rtr = sem("maxima_transposed")
        s_m = sem("row_max_steps")
        s_mb = sem("row_max_spread")
        s_e0 = sem("exp_neg_max_ready")
        s_etok = sem("masked_weight_steps")
        s_res = sem("residual_copied")
        s_dend = sem("den_high_steps")
        s_dtok = sem("den_token_product")
        s_rec = sem("den_reciprocal_steps")
        s_b = sem("shift_ready")
        s_shift = sem("score_unit_shifted")
        s_exp = sem("score_unit_exp")
        s_den = sem("den_steps")
        s_z = sem("subset_sum_steps")
        s_ec = sem("masked_terms_ready")
        s_pv = sem("pv_done")
        s_denb = sem("den_spread")
        s_fin = sem("attention_norm_steps")
        s_op = sem("out_projection_ready")
        s_lin = sem("ln_input_ready")
        s_lmean = sem("ln_mean_ready")
        s_lcen = sem("ln_centred")
        s_lsq = sem("ln_squared")
        s_lvar = sem("ln_variance_ready")
        s_lln = sem("ln_log_ready")
        s_lstd = sem("ln_rstd_ready")
        s_lnorm = sem("ln_normed")
        s_lout = sem("ln_output_ready")
        s_w1 = sem("ffn_up_ready")
        s_gelu = sem("gelu_ready")
        s_w2 = sem("ffn_down_ready")
        s_x2 = sem("residual_ready")
        s_gate = sem("gate_product_ready")
        s_gexp = sem("gate_exp_ready")
        s_gv = sem("gate_vector_steps")
        s_ctp = sem("combine_transposed")
        s_ctc = sem("combine_copied")
        s_gu = sem("expert_up_ready")
        s_cb = sem("combine_spread")
        s_sg = sem("expert_silu_ready")
        s_act = sem("expert_hidden_ready")
        s_hvs = sem("expert_hidden_steps")
        s_eo = sem("expert_out_ready")
        s_od = sem("expert_out_copied")
        s_out = sem("out_stored")
        ONE = 1
        STARTED = (s_res, s_vst, s_lout, s_pv, s_pe, s_hst, s_free, s_x2, s_act, s_od, s_out)
        block = ctx.enter_context(nc.Block())

        MOD_STEPS, GATE_STEPS = 4, 1
        PRE_LN, ITER_LN = 2 * BATCH, 4
        K_U, Q_U, V_U = (0, 1), (2,), (3,)
        S_U = 4
        RING = S_U + SUNITS
        TILE_COLS = [slice(c * 128, (c + 1) * 128) for c in range(SEQ // 128)]
        assert RING % 2 == 0 and UNIT == SEQ

        def unit_spans(u):
            out = []
            for _, col, n in in_unit(u):
                if out and out[-1][1] == col - u * UNIT:
                    out[-1][1] += n
                else:
                    out.append([col - u * UNIT, col - u * UNIT + n])
            return out

        def chain(engine, signal, start=0):
            done = [start]

            def step(ins):
                ins.then_inc(signal, 1)
                done[0] += 1
                engine.wait_ge(signal, done[0])
            step.count = done
            return step

        def units_of_half(half):
            return [p for p in PLACE if (p[0] >= BLOCKS // 2) == half]

        def in_unit(u):
            return [p for p in PLACE if u * UNIT <= p[1] < (u + 1) * UNIT]

        MAXP = [(u, col, off, n, rs) for u in range(SUNITS) for j, col, nj in in_unit(u)
                for off, n, rs in pieces(j, nj)]
        NMAX = len(MAXP)
        LOWP = [p for p in MAXP if p[1] < GAP[1]]
        HIGHP = [p for p in MAXP if p[1] >= GAP[1]]

        PE_SLOT = {1: ["mean0"], 3: ["var0"], 6: ["up00"], 7: ["up01"], 8: ["down0"], 9: ["up10"], 10: ["up11"],
                   11: ["down1"], 12: ["mean2"], 14: ["var2"]}
        DVE_SLOT = {0: ["add_att"], 1: ["centre0"], 4: ["norm0"], 8: ["add_ffn0"], 11: ["add_ffn1"], 12: ["centre2"],
                    15: ["norm2"]}
        ACT_SLOT = {2: ["square0"], 4: ["rstd0"], 5: ["affine0"], 6: ["gelu00"], 7: ["gelu01"], 9: ["gelu10"],
                    10: ["gelu11"], 13: ["square2"], 15: ["rstd2"], 16: ["affine2"]}

        @block.sync
        def _(sp):
            for s in STARTED:
                sp.sem_inc(s, ONE)
            for dst, src in ((ident, ident_c), (mean_w, mean_c), (neg, neg_c), (cnt, cnt_c), (sel, sel_c),
                             (floor, floor_c), (lnf_s, lnf)):
                sp.dma_start(dst[:], src).then_inc(s_const, 16)
            sp.dma_start(s_c, c_t).then_inc(s_modw, 16)
            sp.dma_start(s_wmod, wmod.rearrange("p (m n) -> p m n", m=6)).then_inc(s_modw, 16)
            sp.dma_start(s_pe_view, pe_t).then_inc(s_modw, 16)
            with sp.Fori(0, BATCH) as b:
                sp.wait_ge(s_pe, ONE + b * 2)
                sp.dma_start(h_in[:], x_t[bass.ds(b, 1)].rearrange("a p n -> p (a n)")).then_inc(s_x, 16)
                sp.wait_ge(s_pe, ONE + b * 2 + 2)
                sp.dma_start(h_dram[bass.ds(b, 1)].rearrange("a p n -> p (a n)"), att[:]).then_inc(s_hst, 16)
            sp.wait_ge(s_hst, ONE + 16 * BATCH)
            with sp.Fori(0, LAYERS) as l:
                with sp.Fori(0, BATCH) as b:
                    it = l * BATCH + b
                    sp.wait_ge(s_vst, ONE + it * 16)
                    sp.dma_start(wa_s[:], wa[bass.ds(l, 1)].rearrange("a p n -> p (a n)")).then_inc(s_wa, 16)
                    sp.wait_ge(s_hst, ONE + it * 16 + 16)
                    sp.wait_ge(s_res, ONE + it * 2)
                    sp.dma_start(h_in[:], h_dram[bass.ds(it, 1)].rearrange("a p n -> p (a n)")).then_inc(s_h, 16)
                    sp.wait_ge(s_zero, 3)
                    sp.wait_ge(s_pv, ONE + it)
                    sp.wait_ge(s_free, ONE + it * RING + K_U[1] + 1)
                    for h in range(HEADS):
                        p = slice(h * HD, (h + 1) * HD)
                        sp.dma_start(diag[p, 0:2, h * LO:(h + 1) * LO, :],
                                     k_t[p, :].rearrange("p (a l j) -> p a l j", a=2, l=LO)).then_inc(s_kx, 16)
                    sp.wait_ge(s_free, ONE + it * RING + V_U[0] + 1)
                    sp.dma_start(v_dram, n_t[:]).then_inc(s_vst, 16)
                    sp.wait_ge(s_vst, ONE + it * 16 + 16)
                    for half, slot, s in ((0, 2, s_vx0), (1, 0, s_vx1)):
                        if half:
                            sp.wait_ge(s_sdone, it + 1)
                        for h in range(HEADS):
                            src = v_dram[h * HD:(h + 1) * HD, :].rearrange("d (l j) -> l d j", l=LO)
                            sp.dma_start(diag[h * LO:(h + 1) * LO, slot, h * HD:(h + 1) * HD, :],
                                         src[:, :, half * BLOCKS // 2:(half + 1) * BLOCKS // 2]).then_inc(s, 16)
                    sp.wait_ge(s_lout, ONE + it * ITER_LN + PRE_LN)
                    sp.dma_start(wb_s[:], wb[bass.ds(l, 1)].rearrange("a p n -> p (a n)")).then_inc(s_wb, 16)
            sp.wait_ge(s_hst, ONE + 16 * (BATCH + ITERS))
            for dst, src in ((e_w1, we1), (e_w3, we3), (e_w2, we2), (e_tri, tri_c), (e_ind, ind_c)):
                sp.dma_start(dst, src).then_inc(s_modw, 16)
            sp.dma_start(e_wg, w_gate).then_inc(s_modw, 16)
            with sp.Fori(0, BATCH) as b:
                sp.wait_ge(s_x2, ONE + b * 2)
                sp.dma_start(h_in[:], h_dram[bass.ds(b + ITERS, 1)].rearrange("a p n -> p (a n)")).then_inc(s_h, 16)
                sp.dma_start(x2[:, bass.ds(b * SEQ, SEQ)], x_t[bass.ds(b, 1)].rearrange("a p n -> p (a n)"))\
                    .then_inc(s_x, 16)
            with sp.Fori(0, BATCH) as b:
                for t in range(2):
                    sp.wait_ge(s_od, ONE + b * 4 + 2 * t + 2)
                    sp.dma_start(out[bass.ds(b, 1), :, t * HALF:(t + 1) * HALF].rearrange("a p n -> p (a n)"),
                                 out_s[:, t, :]).then_inc(s_out, 16)
            sp.wait_ge(s_out, ONE + 16 * 2 * BATCH)

        @block.tensor
        def _(pe):
            mm = nc.tensor.matmul

            def ln_mean(n, src, t):
                cols = slice(t * HALF, (t + 1) * HALF)
                mm(acc[:, cols], mean_w[:], src[:, cols], start=True, stop=True).then_inc(s_lmean, 1)

            def ln_variance(n, t):
                cols = slice(t * HALF, (t + 1) * HALF)
                pe.wait_ge(s_lsq, n + 1)
                mm(acc[:, cols], mean_w[:], h_sq[:, cols], start=True, stop=True).then_inc(s_lvar, 1)

            def layer_norm(n, src, written=None):
                for t in range(2):
                    if written is not None:
                        pe.wait_ge(s_lin, written + t + 1)
                    ln_mean(n + t, src, t)
                for t in range(2):
                    ln_variance(n + t, t)

            pe.wait_ge(s_modw, 48)
            pe.wait_ge(s_silu, 1)
            for m in range(6):
                last = mm(acc[:, m * BATCH:(m + 1) * BATCH], s_wmod[:, m, :], s_sig, start=True, stop=True)
            last.then_inc(s_modp, 1)
            pe.wait_ge(s_const, 16 * 7)
            pe.wait_ge(s_modv, 1)
            with pe.Fori(0, BATCH) as b:
                pe.wait_ge(s_x, b * 16 + 16)
                layer_norm(b * 2, h_in)

            def tail(i, step):
                n = i * ITER_LN + PRE_LN
                name, arg = step[:-1], int(step[-1])
                if name == "project":
                    pe.wait_ge(s_wb, i * 16 + 16)
                    pe.wait_ge(s_fin, i * 2 + 2)
                    for t in range(2):
                        mm(acc[:, t * HALF:(t + 1) * HALF], wo, att[:, t * HALF:(t + 1) * HALF],
                           start=True, stop=True).then_inc(s_op, 1)
                elif name == "mean":
                    for t in range(2):
                        pe.wait_ge(s_lin, i * ITER_LN + arg + t + 1)
                        ln_mean(n + arg + t, res, t)
                elif name == "var":
                    for t in range(2):
                        ln_variance(n + arg + t, t)
                elif name[:2] == "up":
                    t, p = int(step[2]), arg
                    pe.wait_ge(s_lout, ONE + n + 2)
                    if t or p:
                        pe.wait_ge(s_gelu, i * 2 * FCH + FCH * t + 2 * p)
                    if t and not p:
                        pe.wait_ge(s_lin, i * ITER_LN + 3)
                    for c in range(2):
                        mm(acc[:, c * HALF:(c + 1) * HALF], w1[:, 2 * p + c, :], att[:, t * HALF:(t + 1) * HALF],
                           start=True, stop=True).then_inc(s_w1, 1)
                else:
                    t = arg
                    pe.wait_ge(s_gelu, i * 2 * FCH + FCH * (t + 1))
                    for c in range(FCH):
                        last = mm(acc[:, t * HALF:(t + 1) * HALF], w2[:, c, :], gl[:, c, :],
                                  start=(c == 0), stop=(c == FCH - 1))
                    last.then_inc(s_w2, 1)

            def iteration(it, with_tail):
                def take(u):
                    pe.wait_ge(s_free, ONE + it * RING + max(u - 1, 0))
                    return ring[:, u % 2, :]

                pe.wait_ge(s_wa, it * 16 + 16)
                pe.wait_ge(s_h, it * 16 + 16)
                for t in range(2):
                    dst = take(K_U[t])
                    mm(dst[:, 0:HALF], wa_s[:, D:2 * D], h_in[:, t * HALF:(t + 1) * HALF],
                       start=True, stop=True).then_inc(s_full, 1)
                for u, w in ((Q_U[0], 0), (V_U[0], 2)):
                    dst = take(u)
                    for t in range(2):
                        last = mm(dst[:, t * HALF:(t + 1) * HALF], wa_s[:, w * D:(w + 1) * D],
                                  h_in[:, t * HALF:(t + 1) * HALF], start=True, stop=True)
                    last.then_inc(s_full, 1)
                if with_tail:
                    tail(it - 1, "project0")
                pe.wait_ge(s_kx, it * 256 + 256)
                pe.wait_ge(s_free, ONE + it * RING + Q_U[0] + 1)
                for u in range(SUNITS):
                    dst = take(S_U + u)
                    for j, col, nj in in_unit(u):
                        if j == BLOCKS // 2:
                            last.then_inc(s_sdone, 1)
                        jh, jr = divmod(j, BLOCKS // 2)
                        keys = diag[:, jh, :, jr]
                        for top in ((0, 1) if nj > HALF else (None,)):
                            for off, n, rs in pieces(j, nj, fixed_top=top):
                                c = col - u * UNIT + off
                                last = mm(view_block(dst[:, c:c + n], rs), keys, view_queries(q_t[:], rs),
                                          start=True, stop=True)
                        if (j, col, nj) == in_unit(u)[-1]:
                            last.then_inc(s_full, 1)
                    if with_tail:
                        for step in PE_SLOT.get(u, ()):
                            tail(it - 1, step)
                pe.wait_ge(s_max, it * (NMAX + 1) + NMAX + 1)
                if with_tail:
                    pe.wait_ge(s_lnorm, it * ITER_LN + PRE_LN)
                for cols in TILE_COLS:
                    last = nc.tensor.transpose(acc[:, cols], q_t[:, cols], ident[:])
                last.then_inc(s_rtr, 1)
                pe.wait_ge(s_m, it * 4 + 4)
                for cols in TILE_COLS:
                    last = nc.tensor.transpose(red[:, cols], q_t[:, cols], ident[:])
                last.then_inc(s_mb, 1)
                pe.wait_ge(s_vx0, it * 256 + 256)
                for u in range(SUNITS):
                    pe.wait_ge(s_exp, it * SUNITS + u + 1)
                    for j, col, nj in in_unit(u):
                        if j == BLOCKS // 2:
                            pe.wait_ge(s_vx1, it * 256 + 256)
                        jh, jr = divmod(j, BLOCKS // 2)
                        vals = diag[:, 2 if jh == 0 else 0, :, jr]
                        for top in (0, 1):
                            for off, n, rs in pieces(j, nj, fixed_top=top):
                                last = mm(view_queries(acc[:], rs), vals,
                                          view_block(score[:, col + off:col + off + n], rs),
                                          start=(j == 0), stop=(j == LAST_HIGH or (j == LAST_LOW and top == 1)),
                                          skip_group_check=True)
                last.then_inc(s_pv, 1)
                pe.wait_ge(s_den, it * len(LOWP) + len(LOWP))
                pe.wait_ge(s_dend, it * (len(HIGHP) + 1) + len(HIGHP) + 1)
                for c, cols in enumerate(TILE_COLS):
                    last = mm(red[:, c * HEADS:(c + 1) * HEADS], q_t[:, cols], sel[:], start=True, stop=True)
                last.then_inc(s_dtok, 1)
                pe.wait_ge(s_rec, it * 3 + 3)
                for cols in TILE_COLS:
                    last = nc.tensor.transpose(red[:, cols], q_t[:, cols], ident[:])
                last.then_inc(s_denb, 1)

            iteration(0, False)
            with pe.Fori(1, ITERS) as it:
                iteration(it, True)
            tail(ITERS - 1, "project0")
            for u in range(SUNITS):
                for step in PE_SLOT.get(u, ()):
                    tail(ITERS - 1, step)

            base = PRE_LN + ITERS * ITER_LN
            with pe.Fori(0, BATCH) as b:
                pe.wait_ge(s_h, (ITERS + 1) * 16 + b * 16)
                pe.wait_ge(s_lnorm, base + b * 4)
                layer_norm(base + b * 4, h_in)
                layer_norm(base + b * 4 + 2, res, ITERS * ITER_LN + b * 2)
            pe.wait_ge(s_modw, 48 + 96)
            pe.wait_ge(s_lout, ONE + base + 4 * BATCH)
            for c in range(TILES):
                last = mm(acc[:, c * EXPERTS:(c + 1) * EXPERTS], hm[:, c * 128:(c + 1) * 128], e_wg,
                          start=True, stop=True)
            last.then_inc(s_gate, 1)
            pe.wait_ge(s_gv, GATE_STEPS)
            for r in range(4):
                if r >= 2:
                    pe.wait_ge(s_ctc, r - 1)
                for c in range(8):
                    k = r * 8 + c
                    last = nc.tensor.transpose(ring[0:EXPERTS, r % 2, c * 128:(c + 1) * 128],
                                               m_a[:, k * EXPERTS:(k + 1) * EXPERTS], ident[:])
                last.then_inc(s_ctp, 1)
            pe.wait_ge(s_ctc, 4)
            with pe.Fori(0, BATCH) as b:
                for t in range(2):
                    for c in range(MCH + 1):
                        if c < MCH:
                            n = 2 * MCH * b + t * MCH + c
                            q = (t * MCH + c) % 2
                            rhs = hm[:, bass.ds(b * SEQ + t * HALF, HALF)]
                            pe.wait_ge(s_act, ONE + (n - 1 if t or c else n))
                            mm(ring[:, q, 0:HALF], e_w1[:, c, :], rhs, start=True, stop=True)
                            mm(ring[:, q, HALF:UNIT], e_w3[:, c, :], rhs, start=True, stop=True).then_inc(s_gu, 1)
                            if c < MCH - 1:
                                mm(red[:, q * HALF:(q + 1) * HALF], e_ind[:, c, :],
                                   comb_t[:, bass.ds(b * SEQ + t * HALF, HALF)], start=True, stop=True)\
                                    .then_inc(s_cb, 1)
                        if c >= 1:
                            n = 2 * MCH * b + t * MCH + c - 1
                            pe.wait_ge(s_act, ONE + n + 1)
                            if c == 1:
                                pe.wait_ge(s_od, ONE + b * 4)
                            last = mm(acc[:, t * HALF:(t + 1) * HALF], e_w2[:, c - 1, :],
                                      m_z[:, (t * MCH + c - 1) % 2, :], start=(c == 1), stop=(c == MCH))
                    last.then_inc(s_eo, 1)

        @block.scalar
        def _(act):
            A = nc.scalar.activation

            def ln_square(n, t):
                cols = slice(t * HALF, (t + 1) * HALF)
                act.wait_ge(s_lcen, n + 1)
                A(h_sq[:, cols], res[:, cols], ACT.Square).then_inc(s_lsq, 1)

            def ln_rstd(n):
                for t in range(2):
                    act.wait_ge(s_lvar, n + t + 1)
                    A(acc[:, t * HALF:(t + 1) * HALF], acc[:, t * HALF:(t + 1) * HALF], ACT.Ln, bias=eps[:])\
                        .then_inc(s_lln, 1)
                for t in range(2):
                    act.wait_ge(s_lln, n + t + 1)
                    A(acc[:, t * HALF:(t + 1) * HALF], acc[:, t * HALF:(t + 1) * HALF], ACT.Exp, scale=-0.5)\
                        .then_inc(s_lstd, 1)

            def ln_affine(n, t, dst, g, beta):
                cols = slice(t * HALF, (t + 1) * HALF)
                act.wait_ge(s_lnorm, n + 1)
                A(dst[:, cols] if not isinstance(dst, list) else dst[t], h_sq[:, cols], ACT.Identity,
                  scale=g, bias=beta).then_inc(s_lout, 1)

            def layer_norm(n, dst, g, beta):
                for t in range(2):
                    ln_square(n + t, t)
                ln_rstd(n)
                for t in range(2):
                    ln_affine(n + t, t, dst, g, beta)

            act.wait_ge(s_modw, 48)
            A(s_sgn[:, 0:BATCH], s_c, ACT.Exp, scale=-1.0).then_inc(s_silu_e, 1)
            act.wait_ge(s_modv, MOD_STEPS)
            act.wait_ge(s_eps, 2)
            act.wait_ge(s_const, 16 * 7)
            with act.Fori(0, BATCH) as b:
                act.wait_ge(s_lout, ONE + b * 2)
                A(cur[:], mod[:, :, bass.ds(b, 1)].rearrange("p m a -> p (m a)"), ACT.Copy).then_inc(s_cur, 1)
                act.wait_ge(s_cur, b + 1)
                act.wait_ge(s_pe, ONE + b * 2)
                act.wait_ge(s_hst, ONE + b * 16)
                layer_norm(b * 2, att, cur[:, 1:2], cur[:, 0:1])

            def tail(i, step):
                n = i * ITER_LN + PRE_LN
                arg = int(step[-1])
                if step.startswith("square"):
                    for t in range(2):
                        ln_square(n + arg + t, t)
                elif step.startswith("rstd"):
                    ln_rstd(n + arg)
                elif step.startswith("gelu"):
                    t, p = int(step[4]), arg
                    if t and not p:
                        act.wait_ge(s_w2, i * 2 + 1)
                    if not t and not p:
                        act.wait_ge(s_lout, ONE + n + 2)
                    for c in range(2):
                        k = 2 * p + c
                        act.wait_ge(s_w1, i * 2 * FCH + FCH * t + k + 1)
                        A(gl[:, k, :], acc[:, c * HALF:(c + 1) * HALF], ACT.Gelu, bias=b1[k]).then_inc(s_gelu, 1)
                else:
                    g, beta = (g2, be2) if arg else (g1, be1)
                    for t in range(2):
                        ln_affine(n + arg + t, t, att, g, beta)
                    if arg:
                        act.wait_ge(s_lout, ONE + n + ITER_LN)
                        act.dma_start(h_dram[bass.ds(i + BATCH, 1)].rearrange("a p n -> p (a n)"), att[:])\
                            .then_inc(s_hst, 16)

            def iteration(it, with_tail):
                act.wait_ge(s_wa, it * 16 + 16)
                if with_tail:
                    act.wait_ge(s_ec, it)
                    act.wait_ge(s_denb, it)
                    act.wait_ge(s_fin, it * 2 - 1)
                for t in range(2):
                    act.wait_ge(s_full, it * RING + K_U[t] + 1)
                    A(k_t[:, t * HALF:(t + 1) * HALF].rearrange("p (l j) -> p j l", l=LO),
                      ring[:, K_U[t] % 2, 0:HALF].rearrange("p (j l) -> p j l", l=LO), ACT.Identity, bias=bk)\
                        .then_inc(s_free, 1)
                act.wait_ge(s_full, it * RING + Q_U[0] + 1)
                A(q_t[:], ring[:, Q_U[0] % 2, :], ACT.Identity, bias=bq).then_inc(s_free, 1)
                act.wait_ge(s_full, it * RING + V_U[0] + 1)
                A(n_t[:].rearrange("p (l j) -> p j l", l=LO),
                  ring[:, V_U[0] % 2, :].rearrange("p (j l) -> p j l", l=LO), ACT.Identity, bias=bv)\
                    .then_inc(s_free, 1)
                for u in range(SUNITS):
                    act.wait_ge(s_full, it * RING + S_U + u + 1)
                    for a, z in unit_spans(u):
                        last = A(score[:, u * UNIT + a:u * UNIT + z], ring[:, (S_U + u) % 2, a:z], ACT.Copy,
                                 scale=SCALE)
                    last.then_inc(s_free, 1)
                    if with_tail:
                        for step in ACT_SLOT.get(u, ()):
                            tail(it - 1, step)
                act.wait_ge(s_m, it * 4 + 3)
                A(e_tok[:], m_tok[:], ACT.Exp, scale=-1.0).then_inc(s_etok, 1)
                act.wait_ge(s_mb, it + 1)
                act.wait_ge(s_z, it * 11 + 11)
                A(n_t[:], red[:], ACT.Exp, scale=-1.0).then_inc(s_e0, 1)
                for u in range(SUNITS):
                    act.wait_ge(s_shift, it * SUNITS + u + 1)
                    for a, z in unit_spans(u):
                        last = A(score[:, u * UNIT + a:u * UNIT + z], score[:, u * UNIT + a:u * UNIT + z], ACT.Exp)
                    last.then_inc(s_exp, 1)
                    if u == 2:
                        act.wait_ge(s_h, it * 16 + 16)
                        A(res[:], h_in[:], ACT.Copy).then_inc(s_res, 2)

            iteration(0, False)
            with act.Fori(1, ITERS) as it:
                iteration(it, True)
            for u in range(SUNITS):
                for step in ACT_SLOT.get(u, ()):
                    tail(ITERS - 1, step)

            base = PRE_LN + ITERS * ITER_LN
            with act.Fori(0, BATCH) as b:
                act.wait_ge(s_lout, ONE + base + b * 4)
                act.wait_ge(s_x2, ONE + b * 2)
                A(cur[:], mod[:, :, bass.ds(b, 1)].rearrange("p m a -> p (m a)"), ACT.Copy).then_inc(s_cur, 1)
                act.wait_ge(s_cur, BATCH + b + 1)
                layer_norm(base + b * 4, att, lnf_s[:, 0:1], lnf_s[:, 1:2])
                layer_norm(base + b * 4 + 2, [hm[:, bass.ds(b * SEQ + t * HALF, HALF)] for t in range(2)],
                           cur[:, 4:5], cur[:, 3:4])
            act.wait_ge(s_gate, 1)
            A(m_a, acc[:, 0:512], ACT.Exp, scale=-1.0).then_inc(s_gexp, 1)
            for r in range(4):
                act.wait_ge(s_ctp, r + 1)
                A(comb_t[:, r * SEQ:(r + 1) * SEQ], ring[0:EXPERTS, r % 2, :], ACT.Copy).then_inc(s_ctc, 1)
            with act.Fori(0, BATCH) as b:
                act.wait_ge(s_od, ONE + b * 4)
                A(cur[:], mod[:, :, bass.ds(b, 1)].rearrange("p m a -> p (m a)"), ACT.Copy).then_inc(s_cur, 1)
                for t in range(2):
                    for c in range(MCH):
                        n = 2 * MCH * b + t * MCH + c
                        q = (t * MCH + c) % 2
                        act.wait_ge(s_gu, n + 1)
                        act.wait_ge(s_act, ONE + (n - 1 if t or c else n))
                        A(m_sg[:, q, :], ring[:, q, 0:HALF], ACT.Silu).then_inc(s_sg, 1)

        @block.vector
        def _(dve):
            V = nc.vector

            def ln_centre(n, src, t):
                cols = slice(t * HALF, (t + 1) * HALF)
                dve.wait_ge(s_lmean, n + 1)
                V.tensor_tensor(res[:, cols], src[:, cols], acc[:, cols], ALU.subtract).then_inc(s_lcen, 1)

            def ln_norm(n, t):
                cols = slice(t * HALF, (t + 1) * HALF)
                dve.wait_ge(s_lstd, n + 1)
                V.tensor_tensor(h_sq[:, cols], acc[:, cols], res[:, cols], ALU.mult).then_inc(s_lnorm, 1)

            def layer_norm(n, src):
                for t in range(2):
                    ln_centre(n + t, src, t)
                for t in range(2):
                    ln_norm(n + t, t)

            for a in range(3):
                V.memset(diag[:, a, :, :], 0.0).then_inc(s_zero, 1)
            V.memset(eps[:], EPS).then_inc(s_eps, 1)
            V.memset(one[:], 1.0).then_inc(s_eps, 1)
            mv = chain(dve, s_dv)
            dve.wait_ge(s_silu_e, 1)
            mv(V.tensor_scalar(s_sgn[:, 0:BATCH], s_sgn[:, 0:BATCH], 1.0, None, ALU.add))
            mv(V.reciprocal(s_sgn[:, 0:BATCH], s_sgn[:, 0:BATCH]))
            V.tensor_tensor(s_sig, s_c, s_sgn[:, 0:BATCH], ALU.mult).then_inc(s_silu, 1)
            dve.wait_ge(s_modp, 1)
            V.tensor_copy(mod[:], acc[:, 0:6 * BATCH].rearrange("p (m b) -> p m b", m=6)).then_inc(s_modv, 1)
            dve.wait_ge(s_modv, 1)
            dve.wait_ge(s_silu, 1)
            for m in (1, 4):
                V.tensor_scalar(mod[:, m, :], mod[:, m, :], 1.0, None, ALU.add).then_inc(s_modv, 1)
            for m in (2, 5):
                mv(V.tensor_scalar(s_sgn[:, 0:BATCH], mod[:, m, :], 0.0, 2.0, ALU.is_ge, ALU.mult))
                mv(V.tensor_scalar(s_sgn[:, BATCH:2 * BATCH], mod[:, m, :], -1.0, 0.25, ALU.mult, ALU.max))
                mv(V.tensor_tensor(s_sgn[:, BATCH:2 * BATCH], s_sgn[:, BATCH:2 * BATCH], mod[:, m, :], ALU.max))
                mv(V.tensor_scalar(s_sgn[:, 0:BATCH], s_sgn[:, 0:BATCH], -1.0, None, ALU.add))
                mv(V.tensor_tensor(mod[:, m, :], s_sgn[:, 0:BATCH], s_sgn[:, BATCH:2 * BATCH], ALU.mult)) \
                    if m == 2 else V.tensor_tensor(mod[:, m, :], s_sgn[:, 0:BATCH], s_sgn[:, BATCH:2 * BATCH],
                                                   ALU.mult).then_inc(s_modv, 1)
            assert MOD_STEPS == 4
            dve.wait_ge(s_modw, 48)
            with dve.Fori(0, BATCH) as b:
                dve.wait_ge(s_x, b * 16 + 16)
                layer_norm(b * 2, h_in)
                for t in range(2):
                    cols = slice(t * HALF, (t + 1) * HALF)
                    dve.wait_ge(s_lout, ONE + b * 2 + t + 1)
                    V.tensor_tensor(att[:, cols], att[:, cols], s_pe_view[:, cols], ALU.add).then_inc(s_pe, 1)

            def tail(i, step):
                n = i * ITER_LN + PRE_LN
                if step == "add_att":
                    for t in range(2):
                        cols = slice(t * HALF, (t + 1) * HALF)
                        dve.wait_ge(s_op, i * 2 + t + 1)
                        V.scalar_tensor_tensor(out=res[:, cols], in0=acc[:, cols], scalar=bo, in1=res[:, cols],
                                               op0=ALU.add, op1=ALU.add).then_inc(s_lin, 1)
                elif step.startswith("add_ffn"):
                    t = int(step[-1])
                    cols = slice(t * HALF, (t + 1) * HALF)
                    dve.wait_ge(s_w2, i * 2 + t + 1)
                    V.scalar_tensor_tensor(out=res[:, cols], in0=acc[:, cols], scalar=b2, in1=att[:, cols],
                                           op0=ALU.add, op1=ALU.add).then_inc(s_lin, 1)
                else:
                    arg = int(step[-1])
                    for t in range(2):
                        if step.startswith("centre"):
                            ln_centre(n + arg + t, res, t)
                        else:
                            ln_norm(n + arg + t, t)

            def iteration(it, with_tail):
                base = it * (NMAX + 1)
                for k, (u, col, off, n, rs) in enumerate(MAXP):
                    if k == 0 or MAXP[k - 1][0] != u:
                        dve.wait_ge(s_free, ONE + it * RING + S_U + u + 1)
                    if k:
                        dve.wait_ge(s_max, base + k)
                    s = view_block(score[:, col + off:col + off + n], rs)
                    r = view_queries(red[:], rs)
                    if k == 0:
                        V.tensor_copy(r, s).then_inc(s_max, 1)
                    else:
                        V.tensor_tensor(r, r, s, ALU.max).then_inc(s_max, 1)
                    if with_tail and (k == NMAX - 1 or MAXP[k + 1][0] != u):
                        for step in DVE_SLOT.get(u, ()):
                            tail(it - 1, step)
                dve.wait_ge(s_max, base + NMAX)
                neg_b = neg[:].unsqueeze(1).broadcast_to([128, BLOCKS, LO])
                V.tensor_tensor(q_t[:].rearrange("p (i l) -> p i l", l=LO),
                                red[:].rearrange("p (i l) -> p i l", l=LO), neg_b, ALU.add).then_inc(s_max, 1)
                dve.wait_ge(s_rtr, it + 1)
                V.tensor_reduce(m_tok[:], acc[:].rearrange("p (g l) -> p g l", l=LO), AX_X, ALU.max)\
                    .then_inc(s_m, 1)
                dve.wait_ge(s_m, it * 4 + 1)
                V.tensor_scalar(m_tok[:, 0:HEADS], m_tok[:, 0:HEADS], floor[:], None, ALU.max).then_inc(s_m, 1)
                V.tensor_scalar(m_tok[:, HEADS:], m_tok[:, HEADS:], 0.0, None, ALU.max).then_inc(s_m, 1)
                dve.wait_ge(s_m, it * 4 + 3)
                lanes = q_t[:].rearrange("p (g l) -> p g l", l=LO)
                V.tensor_copy(lanes, m_tok[:].unsqueeze(2).broadcast_to([128, BLOCKS, LO])).then_inc(s_m, 1)
                dve.wait_ge(s_etok, it * 2 + 1)
                V.tensor_tensor(e_tok[:].rearrange("p (c h) -> p c h", h=HEADS),
                                e_tok[:].rearrange("p (c h) -> p c h", h=HEADS),
                                cnt[:].unsqueeze(2).broadcast_to([128, SEQ // 128, HEADS]), ALU.mult)\
                    .then_inc(s_etok, 1)
                dve.wait_ge(s_e0, it + 1)
                red_v = red[:].rearrange("p (i l) -> p i l", l=LO)
                V.scalar_tensor_tensor(out=red_v, in0=red_v, scalar=-1.0, in1=neg_b, op0=ALU.mult, op1=ALU.add)\
                    .then_inc(s_b, 1)
                dve.wait_ge(s_b, it + 1)
                for k, (u, col, off, n, rs) in enumerate(MAXP):
                    s = view_block(score[:, col + off:col + off + n], rs)
                    last = V.tensor_tensor(s, view_queries(red[:], rs), s, ALU.add)
                    if k == NMAX - 1 or MAXP[k + 1][0] != u:
                        last.then_inc(s_shift, 1)
                base = it * (len(HIGHP) + 1)
                dve.wait_ge(s_shift, it * SUNITS + SUNITS)
                for k, (u, col, off, n, rs) in enumerate(HIGHP):
                    if k == 0 or HIGHP[k - 1][0] != u:
                        dve.wait_ge(s_exp, it * SUNITS + u + 1)
                    if k:
                        dve.wait_ge(s_dend, base + k)
                    s = view_block(score[:, col + off:col + off + n], rs)
                    r = view_queries(red[:], rs)
                    if k == 0:
                        V.tensor_copy(r, s).then_inc(s_dend, 1)
                    else:
                        V.tensor_tensor(r, r, s, ALU.add).then_inc(s_dend, 1)
                dve.wait_ge(s_dend, base + len(HIGHP))
                dve.wait_ge(s_den, it * len(LOWP) + len(LOWP))
                V.tensor_tensor(q_t[:, 0:HALF], red[:, 0:HALF], q_t[:, 0:HALF], ALU.add).then_inc(s_dend, 1)
                dve.wait_ge(s_dtok, it + 1)
                V.tensor_tensor(m_tok[:], red[:, 0:BLOCKS], e_tok[:], ALU.add).then_inc(s_rec, 1)
                dve.wait_ge(s_rec, it * 3 + 1)
                V.reciprocal(m_tok[:], m_tok[:]).then_inc(s_rec, 1)
                dve.wait_ge(s_rec, it * 3 + 2)
                V.tensor_copy(lanes, m_tok[:].unsqueeze(2).broadcast_to([128, BLOCKS, LO])).then_inc(s_rec, 1)
                dve.wait_ge(s_pv, ONE + it + 1)
                dve.wait_ge(s_ec, it + 1)
                dve.wait_ge(s_hst, ONE + it * 16 + 16 * BATCH)
                V.tensor_tensor(att[:], acc[:], k_t[:], ALU.add).then_inc(s_fin, 1)
                dve.wait_ge(s_denb, it + 1)
                dve.wait_ge(s_fin, it * 2 + 1)
                V.tensor_tensor(att[:], red[:], att[:], ALU.mult).then_inc(s_fin, 1)

            iteration(0, False)
            with dve.Fori(1, ITERS) as it:
                iteration(it, True)
            for u in range(SUNITS):
                for step in DVE_SLOT.get(u, ()):
                    tail(ITERS - 1, step)

            base = PRE_LN + ITERS * ITER_LN
            with dve.Fori(0, BATCH) as b:
                dve.wait_ge(s_h, (ITERS + 1) * 16 + b * 16)
                dve.wait_ge(s_lnorm, base + b * 4)
                layer_norm(base + b * 4, h_in)
                dve.wait_ge(s_x, (BATCH + 1) * 16 + b * 16)
                dve.wait_ge(s_cur, BATCH + b + 1)
                for t in range(2):
                    cols = slice(t * HALF, (t + 1) * HALF)
                    dve.wait_ge(s_lout, ONE + base + b * 4 + t + 1)
                    V.scalar_tensor_tensor(out=res[:, cols], in0=att[:, cols], scalar=cur[:, 2:3],
                                           in1=x2[:, bass.ds(b * SEQ + t * HALF, HALF)], op0=ALU.mult,
                                           op1=ALU.add).then_inc(s_x2, 1)
                    dve.wait_ge(s_x2, ONE + b * 2 + t + 1)
                    V.tensor_scalar(x2[:, bass.ds(b * SEQ + t * HALF, HALF)], res[:, cols], 1.0, None, ALU.mult)\
                        .then_inc(s_lin, 1)
                layer_norm(base + b * 4 + 2, res)

            g = chain(dve, s_dv, start=mv.count[0])
            dve.wait_ge(s_gexp, 1)
            dve.wait_ge(s_modw, 48 + 96)
            g(V.tensor_scalar(m_g, m_a, 1.0, None, ALU.add))
            g(V.reciprocal(m_g, m_g))
            s4 = m_g.rearrange("p (q e) -> p q e", e=4)
            hi1, lo1, hi2, lo2 = m_t
            g(V.tensor_tensor(hi1, s4[:, :, 0], s4[:, :, 1], ALU.max))
            g(V.tensor_tensor(lo1, s4[:, :, 0], s4[:, :, 1], ALU.min))
            g(V.tensor_tensor(hi2, s4[:, :, 2], s4[:, :, 3], ALU.max))
            g(V.tensor_tensor(lo2, s4[:, :, 2], s4[:, :, 3], ALU.min))
            g(V.tensor_tensor(m_gs, hi1, hi2, ALU.max))
            g(V.tensor_tensor(hi1, hi1, hi2, ALU.min))
            g(V.tensor_tensor(lo1, lo1, lo2, ALU.max))
            g(V.tensor_tensor(hi1, hi1, lo1, ALU.max))
            g(V.tensor_tensor(m_gs, m_gs, hi1, ALU.add))

            def ranks(dst, val, width):
                n = TILES * width * width
                v = val.rearrange("p (t e) -> p t e", e=width)
                other = v.unsqueeze(2).broadcast_to([128, TILES, width, width])
                own = v.unsqueeze(3).broadcast_to([128, TILES, width, width])
                c1 = m_c1[:, 0:n].rearrange("p (t e o) -> p t e o", t=TILES, e=width)
                c2 = m_c2[:, 0:n].rearrange("p (t e o) -> p t e o", t=TILES, e=width)
                tri = e_tri[:, 0:width, 0:width].unsqueeze(1).broadcast_to([128, TILES, width, width])
                g(V.tensor_tensor(c1, other, own, ALU.is_equal))
                g(V.tensor_tensor(c1, c1, tri, ALU.mult))
                g(V.tensor_tensor(c2, other, own, ALU.is_gt))
                g(V.tensor_tensor(c1, c1, c2, ALU.add))
                g(V.tensor_reduce(dst, m_c1[:, 0:n].rearrange("p (q o) -> p q o", o=width), AX_X, ALU.add))

            ranks(m_al, m_gs, GROUPS)
            g(V.tensor_scalar(m_al, m_al, 1.5, None, ALU.is_lt))
            al = m_al.unsqueeze(2).broadcast_to([128, TILES * GROUPS, 4])
            m_b4 = m_b.rearrange("p (q e) -> p q e", e=4)
            g(V.tensor_tensor(m_b4, s4, al, ALU.mult))
            g(V.tensor_scalar(m_al, m_al, -1.0, None, ALU.add))
            g(V.tensor_tensor(m_b4, m_b4, al, ALU.add))
            ranks(m_a, m_b, EXPERTS)
            g(V.tensor_scalar(m_a, m_a, 3.5, None, ALU.is_lt))
            g(V.tensor_tensor(m_a, m_a, m_g, ALU.mult))
            a3 = m_a.rearrange("p (t e) -> p t e", e=EXPERTS)
            g(V.tensor_reduce(m_t[0][:, 0:TILES], a3, AX_X, ALU.add))
            g(V.tensor_scalar(m_t[0][:, 0:TILES], m_t[0][:, 0:TILES], 1e-6, None, ALU.add))
            g(V.reciprocal(m_t[0][:, 0:TILES], m_t[0][:, 0:TILES]))
            V.tensor_tensor(a3, a3, m_t[0][:, 0:TILES].unsqueeze(2).broadcast_to([128, TILES, EXPERTS]), ALU.mult)\
                .then_inc(s_gv, GATE_STEPS)
            with dve.Fori(0, BATCH) as b:
                dve.wait_ge(s_cur, 2 * BATCH + b + 1)
                for t in range(2):
                    for c in range(MCH):
                        n = 2 * MCH * b + t * MCH + c
                        q = (t * MCH + c) % 2
                        dve.wait_ge(s_sg, n + 1)
                        if c < MCH - 1:
                            V.tensor_tensor(m_y[:, q, :], m_sg[:, q, :], ring[:, q, HALF:UNIT], ALU.mult)\
                                .then_inc(s_hvs, 1)
                            steps = 2 * (MCH - 1) * b + t * (MCH - 1) + c + 1
                            dve.wait_ge(s_hvs, steps)
                            dve.wait_ge(s_cb, steps)
                            V.tensor_tensor(m_z[:, q, :], m_y[:, q, :], red[:, q * HALF:(q + 1) * HALF], ALU.mult)\
                                .then_inc(s_act, 1)
                        else:
                            V.tensor_tensor(m_z[:, q, :], m_sg[:, q, :], ring[:, q, HALF:UNIT], ALU.mult)\
                                .then_inc(s_act, 1)
                    cols = slice(t * HALF, (t + 1) * HALF)
                    dve.wait_ge(s_eo, b * 2 + t + 1)
                    dve.wait_ge(s_out, ONE + b * 32)
                    V.tensor_scalar(out_s[:, t, :], acc[:, cols], cur[:, 5:6], None, ALU.mult).then_inc(s_od, 1)
                    dve.wait_ge(s_od, ONE + b * 4 + 2 * t + 1)
                    V.tensor_tensor(out_s[:, t, :], out_s[:, t, :], x2[:, bass.ds(b * SEQ + t * HALF, HALF)],
                                    ALU.add).then_inc(s_od, 1)

        @block.gpsimd
        def _(pool):
            P = nc.gpsimd
            pool.wait_ge(s_eps, 2)
            pool.wait_ge(s_const, 16 * 7)
            with pool.Fori(0, ITERS) as it:
                zb = it * 11
                pool.wait_ge(s_vst, ONE + it * 16 + 16)
                for k in range(10):
                    v = n_t[:].rearrange("p (a s w) -> p a s w", s=2, w=1 << k)
                    if k:
                        pool.wait_ge(s_z, zb + k)
                    P.tensor_tensor(v[:, :, 1, :], v[:, :, 1, :], v[:, :, 0, :], ALU.add).then_inc(s_z, 1)
                pool.wait_ge(s_z, zb + 10)
                pool.wait_ge(s_kx, it * 256 + 256)
                P.tensor_tensor(k_t[:].rearrange("p (j l) -> p j l", l=LO),
                                n_t[:, SEQ - 1:SEQ].unsqueeze(2).broadcast_to([128, BLOCKS, LO]),
                                n_t[:].rearrange("p (l j) -> p j l", l=LO)[:, ::-1, ::-1], ALU.subtract)\
                    .then_inc(s_z, 1)
                pool.wait_ge(s_e0, it + 1)
                pool.wait_ge(s_z, zb + 11)
                P.tensor_tensor(k_t[:], k_t[:], n_t[:], ALU.mult).then_inc(s_ec, 1)
                base = it * len(LOWP)
                pool.wait_ge(s_mb, it + 1)
                for k, (u, col, off, n, rs) in enumerate(LOWP):
                    if k == 0 or LOWP[k - 1][0] != u:
                        pool.wait_ge(s_exp, it * SUNITS + u + 1)
                    if k:
                        pool.wait_ge(s_den, base + k)
                    s = view_block(score[:, col + off:col + off + n], rs)
                    r = view_queries(q_t[:], rs)
                    if k == 0:
                        P.tensor_tensor(r, s, one[:].broadcast_to([128, n]), ALU.mult).then_inc(s_den, 1)
                    else:
                        P.tensor_tensor(r, r, s, ALU.add).then_inc(s_den, 1)


def _constants():
    import numpy as np
    pos = np.arange(SEQ)
    level = np.frexp((pos + 1).astype(np.float64))[1] - 1
    coord = (pos >> level) / 2.0 ** level
    div = np.exp(np.arange(0, D, 2, dtype=np.float64) * -(np.log(10000.0) / D))
    ang = pos[:, None].astype(np.float64) * div[None, :]
    pe = np.zeros((SEQ, D), np.float32)
    pe[:, 0::2] = (np.sin(ang) * coord[:, None]).astype(np.float32)
    pe[:, 1::2] = (np.cos(ang) * coord[:, None]).astype(np.float32)
    p = np.arange(128)
    lo = np.arange(LO)
    queries = np.arange(SEQ)
    allowed = np.array([1 << (10 - bin(int(i)).count("1")) for i in queries])
    floor = np.zeros((128, 1), np.float32)
    floor[0] = -3e38
    expert = np.arange(EXPERTS)
    chunk = np.arange(MCH - 1)
    ind = expert[:, None, None] == 2 * chunk[None, :, None] + (p // EF)[None, None, :]
    return {
        "pe_t": np.ascontiguousarray(pe.T),
        "ident": np.eye(128, dtype=np.float32),
        "sel": (p[:, None] // LO == np.arange(HEADS)[None, :]).astype(np.float32),
        "mean": np.full((128, 128), 1.0 / D, np.float32),
        "neg": np.where((p[:, None] % LO) & lo[None, :], np.float32(NEG), np.float32(0)).astype(np.float32),
        "cnt": (SEQ - allowed).astype(np.float32).reshape(SEQ // 128, 128).T,
        "floor": floor,
        "tri": np.broadcast_to((expert[None, :] < expert[:, None]).astype(np.float32), (128, 16, 16)).copy(),
        "ind": ind.astype(np.float32),
    }


def kernel(**inputs):
    import numpy as np
    import concourse.bacc as bacc
    from concourse.bass_utils import run_bass_kernel_spmd

    a = {k: np.asarray(v) for k, v in inputs.items()}
    at = {k[8:]: v for k, v in a.items() if k.startswith("L0_attn_")}
    ff = {k[7:]: v for k, v in a.items() if k.startswith("L0_ffn_")}
    col = lambda v: v.reshape(LAYERS, D, 1)
    const = _constants()
    arrays = {
        "x_t": at["x"].transpose(0, 2, 1),
        "pe_t": const["pe_t"],
        "wa": np.concatenate([at["Wq"], at["Wk"], at["Wv"], col(at["bq"]), col(at["bk"]), col(at["bv"])], axis=2),
        "wb": np.concatenate(
            [at["Wo"], at["W1"], at["W2"].reshape(LAYERS, FCH, D, D).transpose(0, 2, 1, 3).reshape(LAYERS, D, HID)]
            + [col(at[k]) for k in ("bo", "b2", "ln1_g", "ln1_b", "ln2_g", "ln2_b")]
            + [at["b1"].reshape(LAYERS, FCH, D).transpose(0, 2, 1)], axis=2),
        "lnf": np.stack([at["lnf_g"], at["lnf_b"]], axis=1),
        "c_t": a["L0_c"].T,
        "wmod": a["L0_wmod"],
        "w_gate": ff["w_gate"].T,
        "we1": np.concatenate([ff["w1_e"].reshape(EXPERTS * EF, D), ff["w1_s"]]).T.reshape(D, MCH, 128),
        "we3": np.concatenate([ff["w3_e"].reshape(EXPERTS * EF, D), ff["w3_s"]]).T.reshape(D, MCH, 128),
        "we2": np.concatenate([ff["w2_e"].transpose(0, 2, 1).reshape(EXPERTS * EF, D), ff["w2_s"].T])
        .reshape(MCH, 128, D).transpose(1, 0, 2),
        "ident": const["ident"], "sel": const["sel"], "mean": const["mean"], "neg": const["neg"],
        "cnt": const["cnt"], "floor": const["floor"], "tri": const["tri"], "ind": const["ind"],
    }
    nc = bacc.Bacc("TRN2", target_bir_lowering=False, num_devices=1)
    feed, args = {}, []
    for name, v in arrays.items():
        feed[f"in_{name}"] = np.ascontiguousarray(v)
        args.append(nc.dram_tensor(f"in_{name}", v.shape, F32, kind="ExternalInput").ap())
    h_dram = nc.dram_tensor("h_scratch", (BATCH + ITERS, D, SEQ), F32, kind="Internal").ap()
    v_dram = nc.dram_tensor("v_scratch", (D, SEQ), F32, kind="Internal").ap()
    out = nc.dram_tensor("out_t", (BATCH, D, SEQ), F32, kind="ExternalOutput").ap()
    adaln_kernel(nc, *args, h_dram, v_dram, out)
    r = run_bass_kernel_spmd(nc, [feed], core_ids=[0])
    return np.ascontiguousarray(r.results[0]["out_t"].transpose(0, 2, 1))
```

```python
from contextlib import ExitStack

import concourse.bass as bass
from concourse import mybir

F32 = mybir.dt.float32
BF16 = mybir.dt.bfloat16
ALU = mybir.AluOpType
ACT = mybir.ActivationFunctionType
AX_X = mybir.AxisListType.X

LAYERS, BATCH, SEQ, D, HEADS, HID = 6, 4, 1024, 128, 16, 512
HD = D // HEADS
LO = 8
BITS = 7
BLOCKS = SEQ // LO
HALF = SEQ // 2
ITERS = LAYERS * BATCH
FCH = HID // D
EPS = 1e-5
NEG = -1e30
SCALE = float(1.0 / (HD ** 0.5))
EXPERTS, GROUPS, EF = 16, 4, 64
MCH = 9
TILES = BATCH * SEQ // 128
PARTS = 3


def block_cols(j):
    return LO << (BITS - bin(j).count("1"))


def packing(js):
    total = sum(block_cols(j) for j in js)
    first = max(block_cols(js[0]) // HALF, 1)
    room = [HALF] * (total // HALF) + [total % HALF]
    banks = [[] for _ in room]
    banks[0] = [js[0]]
    for q in range(first):
        room[q] = 0
    for j in sorted(js[1:], key=lambda j: (-block_cols(j), j)):
        q = max(range(len(room)), key=lambda q: (room[q], q))
        banks[q].append(j)
        room[q] -= block_cols(j)
    assert not any(room)
    mixed = sorted((b for b in banks[first:-1] if len(b) > 1), key=len)
    whole = [b for b in banks[first:-1] if len(b) == 1]
    order = []
    while mixed or whole:
        if mixed:
            order.append(mixed.pop())
        if whole:
            order.append(whole.pop())
    return [j for b in banks[:first] + order + banks[-1:] for j in b]


def placement():
    out, col = [], 0
    for js in (range(BLOCKS // 2), range(BLOCKS // 2, BLOCKS)):
        col = (col + HALF - 1) // HALF * HALF
        for j in packing(js):
            out.append((j, col, block_cols(j)))
            col += block_cols(j)
    return out, col


PLACE, SCORE_COLS = placement()
UNIT = 2 * HALF
SUNITS = (SCORE_COLS + UNIT - 1) // UNIT
GAP = (sum(n for j, _, n in PLACE if j < BLOCKS // 2),
       [c for j, c, _ in PLACE if j == BLOCKS // 2][0])


def pieces(j, n, fixed_top=None, max_runs=2):
    held = {}
    if fixed_top is not None:
        if j >> (BITS - 1) & 1:
            if fixed_top:
                return
        held[BITS - 1] = fixed_top

    def runs(held):
        out = []
        for k in range(BITS - 1, -1, -1):
            kind = "fix" if (j >> k & 1 or k in held) else "free"
            val = held.get(k, 0)
            if out and out[-1][0] == kind and kind == "free":
                out[-1][1] += 1
            elif out and out[-1][0] == kind:
                out[-1] = [kind, out[-1][1] + 1, out[-1][2] * 2 + val]
            else:
                out.append([kind, 1, val])
        return out

    def strided(rs):
        free = [r for r in rs if r[0] == "free"]
        return len(free) - (1 if rs[-1][0] == "free" else 0)

    def split(held):
        rs = runs(held)
        if strided(rs) <= max_runs:
            off = 0
            for k, v in held.items():
                if v:
                    below = sum(1 for q in range(k) if not j >> q & 1)
                    off += LO << below
            cols = LO
            for r in rs:
                if r[0] == "free":
                    cols <<= r[1]
            yield off, cols, rs
            return
        top = max(k for k in range(BITS) if not j >> k & 1 and k not in held)
        yield from split({**held, top: 0})
        yield from split({**held, top: 1})

    yield from split(held)


def view_queries(ap, rs):
    names, sizes, index = [], {}, [slice(None)]
    for q, (kind, bits, val) in enumerate(rs):
        names.append(f"r{q}")
        sizes[f"r{q}"] = 1 << bits
        index.append(slice(None) if kind == "free" else val)
    v = ap.rearrange("p (" + " ".join(names) + " l) -> p " + " ".join(names) + " l", l=LO, **sizes)
    return v[tuple(index) + (slice(None),)]


def view_block(ap, rs):
    free = [(f"r{q}", 1 << bits) for q, (kind, bits, _) in enumerate(rs) if kind == "free"]
    names = " ".join(n for n, _ in free)
    return ap.rearrange(f"p ({names} l) -> p {names} l", l=LO, **dict(free))


def product_order(u):
    blocks = sorted((p for p in PLACE if u * UNIT <= p[1] < (u + 1) * UNIT), key=lambda p: (p[0] >= BLOCKS // 2, -p[2]))
    half = (len(blocks) + 1) // 2
    large, small = blocks[:half], blocks[half:]
    return [p for q in range(half) for p in large[q:q + 1] + small[q:q + 1]]


ORDER = [product_order(u) for u in range(SUNITS)]
LAST_LOW = [j for blocks in ORDER for j, _, _ in blocks if j < BLOCKS // 2][-1]
LAST_HIGH = ORDER[-1][-1][0]
FIRST_HIGH = [j for blocks in ORDER for j, _, _ in blocks if j >= BLOCKS // 2][0]


def adaln_kernel(nc, x_t, pe_t, wa, wb, lnf, c_t, wmod, w_gate, we1, we3, we2,
                 ident_c, sel_c, mean_c, neg_c, cnt_c, floor_c, ind_c,
                 h_dram, v_dram, out):
    with ExitStack() as ctx:
        def sb(name, shape):
            return ctx.enter_context(nc.sbuf_tensor(name, shape, F32))

        def sem(name):
            return ctx.enter_context(nc.semaphore(name))

        ring = ctx.enter_context(nc.psum_tensor("ring", [128, 2, UNIT], F32))
        acc = ctx.enter_context(nc.psum_tensor("acc", [128, SEQ], F32))
        red = ctx.enter_context(nc.psum_tensor("red", [128, SEQ], F32))

        diag = sb("diag", [128, 3, 128, BLOCKS // 2])
        score = sb("score", [128, SCORE_COLS])
        h_in = sb("h_in", [128, SEQ])
        q_t = sb("q_t", [128, SEQ])
        k_t = sb("k_t", [128, SEQ])
        n_t = sb("n_t", [128, SEQ])
        att = sb("att", [128, SEQ])
        res = sb("res", [128, SEQ])
        gl = sb("gl", [128, FCH, HALF])
        h_sq = gl[:, 0:2, :].rearrange("p t n -> p (t n)")
        keys = gl[:, 2:4, :].rearrange("p t n -> p (t n)")
        wa_s = sb("wa_s", [128, 3 * D + 3])
        wb_s = sb("wb_s", [128, D + 2 * HID + 6 + FCH])
        ident = sb("ident", [128, 128])
        mean_w = sb("mean_w", [128, 128])
        neg = sb("neg", [128, LO])
        cnt = sb("cnt", [128, SEQ // 128])
        sel = sb("sel", [128, HEADS])
        floor = sb("floor", [128, 1])
        m_tok = sb("m_tok", [128, BLOCKS])
        e_tok = sb("e_tok", [128, BLOCKS])
        mod = sb("mod", [128, 6, BATCH])
        cur = sb("cur", [128, 6])
        lnf_s = sb("lnf_s", [128, 2])
        eps = sb("eps", [128, 1])
        one = sb("one", [128, 1])

        bq, bk, bv = (wa_s[:, 3 * D + i:3 * D + i + 1] for i in range(3))
        wo = wb_s[:, 0:D]
        w1 = wb_s[:, D:D + HID].rearrange("p (c n) -> p c n", c=FCH)
        w2 = wb_s[:, D + HID:D + 2 * HID].rearrange("p (c n) -> p c n", c=FCH)
        vec = D + 2 * HID
        bo, b2, g1, be1, g2, be2 = (wb_s[:, vec + i:vec + i + 1] for i in range(6))
        b1 = [wb_s[:, vec + 6 + c:vec + 7 + c] for c in range(FCH)]

        s_wmod = score[:, 0:6 * D].rearrange("p (m n) -> p m n", m=6)
        s_c = score[:, 6 * D:6 * D + BATCH]
        s_sig = score[:, 6 * D + BATCH:6 * D + 2 * BATCH]
        s_sgn = score[:, 6 * D + 2 * BATCH:6 * D + 4 * BATCH]
        s_pe_view = score[:, 2 * UNIT:3 * UNIT]
        x_all = score[:, 4 * SEQ:8 * SEQ]
        x_cen = score[:, 8 * SEQ:12 * SEQ]
        x_sq = score[:, 12 * SEQ:16 * SEQ]
        hm = score[:, 0:4 * SEQ]
        x2 = score[:, 4 * SEQ:8 * SEQ]
        m_g = score[:, 8 * SEQ:8 * SEQ + 512]
        m_a = score[:, 8 * SEQ + 512:9 * SEQ]
        m_b = score[:, 9 * SEQ:9 * SEQ + 512]
        m_gs = score[:, 9 * SEQ + 512:9 * SEQ + 640]
        m_al = score[:, 9 * SEQ + 640:9 * SEQ + 768]
        m_t = [score[:, 9 * SEQ + 768 + 128 * i:9 * SEQ + 896 + 128 * i] for i in range(4)]
        out_s = score[:, 15 * SEQ:15 * SEQ + 2 * HALF].rearrange("p (a n) -> p a n", a=2)
        m_sg = score[:, 16 * SEQ:17 * SEQ].rearrange("p (a n) -> p a n", a=2)
        dflat = diag[:, :, :, :].rearrange("p a m j -> p (a m j)")
        m_parts = dflat[:, 8192:8192 + TILES * PARTS * EXPERTS].rearrange("p (t a e) -> p t a e", t=TILES, a=PARTS)
        m_bf = dflat[:, 10 * SEQ:10 * SEQ + 256].bitcast(BF16).rearrange("p (t e) -> p t e", t=TILES)
        comb_t = dflat[0:PARTS * EXPERTS, 11 * SEQ:13 * SEQ].bitcast(BF16)
        e_ind_bf = dflat[0:PARTS * EXPERTS, 13 * SEQ:13 * SEQ + 512].bitcast(BF16).rearrange("p (c n) -> p c n", c=8)
        h_all = dflat[:, 0:4 * SEQ]
        h_cen = dflat[:, 4 * SEQ:8 * SEQ]
        h_nrm = dflat[:, 8 * SEQ:12 * SEQ]
        m_c1 = dflat[:, 0:8192]
        o = 16384
        e_w1 = dflat[:, o:o + MCH * 128].rearrange("p (c n) -> p c n", c=MCH)
        e_w3 = dflat[:, o + 1152:o + 2304].rearrange("p (c n) -> p c n", c=MCH)
        e_w2 = dflat[:, o + 2304:o + 3456].rearrange("p (c n) -> p c n", c=MCH)
        e_wg = dflat[:, o + 3456:o + 3472]
        e_ind = dflat[0:PARTS * EXPERTS, o + 3728:o + 4752].rearrange("p (c n) -> p c n", c=8)
        m_y = dflat[:, o + 4752:o + 5776].rearrange("p (a n) -> p a n", a=2)
        m_z = dflat[:, o + 5776:o + 6800].rearrange("p (a n) -> p a n", a=2)

        s_const = sem("const_loaded")
        s_zero = sem("diag_zeroed")
        s_eps = sem("eps_written")
        s_modw = sem("mod_weights_loaded")
        s_silu_e = sem("silu_exp_ready")
        s_silu = sem("silu_ready")
        s_dv = sem("vector_chain")
        s_rank = sem("gate_comparisons")
        s_modp = sem("mod_product_ready")
        s_modv = sem("mod_vector_steps")
        s_x = [sem(f"x_loaded_{b}") for b in range(BATCH)]
        s_cur = sem("mod_column_copied")
        s_pe = sem("pos_added")
        s_hst = sem("h_stored")
        s_h = sem("h_loaded")
        s_wa = sem("projection_weights_loaded")
        s_wb = sem("ffn_weights_loaded")
        s_full = sem("score_unit_in_ring")
        s_free = sem("score_unit_in_sbuf")
        s_kpr = sem("keys_projected")
        s_vpr = sem("values_projected")
        s_qpr = sem("queries_projected")
        s_kev = sem("keys_in_sbuf")
        s_vev = sem("values_in_sbuf")
        s_qev = sem("queries_in_sbuf")
        s_vst = sem("v_stored")
        s_kx0 = sem("diag_keys_low_loaded")
        s_kx1 = sem("diag_keys_high_loaded")
        s_vx0 = sem("diag_values_low_loaded")
        s_vx1 = sem("diag_values_high_loaded")
        s_max = sem("max_steps")
        s_rtr = sem("maxima_transposed")
        s_m = sem("row_max_steps")
        s_mb = sem("row_max_spread")
        s_mbe = sem("row_max_spread_for_exp")
        s_e0 = sem("exp_neg_max_ready")
        s_etok = sem("masked_weight_steps")
        s_res = sem("residual_copied")
        s_dend = sem("den_high_steps")
        s_dtok = sem("den_token_product")
        s_rec = sem("den_reciprocal_steps")
        s_b = sem("shift_ready")
        s_shift = sem("score_unit_shifted")
        s_exp = sem("score_unit_exp")
        s_den = sem("den_steps")
        s_z = sem("subset_sum_steps")
        s_ec = sem("masked_terms_ready")
        s_pv = sem("pv_done")
        s_denb = sem("den_spread")
        s_fin = sem("attention_norm_steps")
        s_op = sem("out_projection_ready")
        s_lin = sem("ln_input_ready")
        s_lmean = sem("ln_mean_ready")
        s_lcen = sem("ln_centred")
        s_lsq = sem("ln_squared")
        s_lvar = sem("ln_variance_ready")
        s_lln = sem("ln_log_ready")
        s_lstd = sem("ln_rstd_ready")
        s_lnorm = sem("ln_normed")
        s_lout = sem("ln_output_ready")
        s_w1 = sem("ffn_up_ready")
        s_gelu = sem("gelu_ready")
        s_w2 = sem("ffn_down_ready")
        s_x2 = sem("residual_ready")
        s_gate = sem("gate_product_ready")
        s_gexp = sem("gate_exp_ready")
        s_gv = sem("gate_vector_steps")
        s_ctp = sem("combine_transposed")
        s_ctc = sem("combine_copied")
        s_gu = sem("expert_up_ready")
        s_cb = sem("combine_spread")
        s_sg = sem("expert_silu_ready")
        s_act = sem("expert_hidden_ready")
        s_hvs = sem("expert_hidden_steps")
        s_eo = sem("expert_out_ready")
        s_od = sem("expert_out_copied")
        s_out = sem("out_stored")
        ONE = 1
        STARTED = (s_res, s_vst, s_lout, s_pv, s_pe, s_hst, s_free, s_x2, s_act, s_od, s_out,
                   s_vev, s_full, s_vx1, s_fin)
        block = ctx.enter_context(nc.Block())

        MOD_STEPS, GATE_STEPS = 4, 1
        PRE_LN, ITER_LN = 2 * BATCH, 4
        KEYS_AT, VALS_AT = (1, 0), (2, 0)
        TILE_COLS = [slice(c * 128, (c + 1) * 128) for c in range(SEQ // 128)]
        assert SUNITS % 2 == 0 and UNIT == SEQ

        def unit_spans(u):
            out = []
            for _, col, n in in_unit(u):
                if out and out[-1][1] == col - u * UNIT:
                    out[-1][1] += n
                else:
                    out.append([col - u * UNIT, col - u * UNIT + n])
            return out

        def chain(engine, signal, start=0):
            done = [start]

            def step(ins):
                ins.then_inc(signal, 1)
                done[0] += 1
                engine.wait_ge(signal, done[0])
            step.count = done
            return step

        def units_of_half(half):
            return [p for p in PLACE if (p[0] >= BLOCKS // 2) == half]

        def in_unit(u):
            return [p for p in PLACE if u * UNIT <= p[1] < (u + 1) * UNIT]

        MAXP = [(u, col, off, n, rs) for u in range(SUNITS) for j, col, nj in in_unit(u)
                for off, n, rs in pieces(j, nj)]
        NMAX = len(MAXP)
        MAX_STEPS = NMAX + 4
        LOWP = [p for p in MAXP if p[1] < GAP[1]]
        HIGHP = [p for p in MAXP if p[1] >= GAP[1]]

        SPREAD_AFTER = 0
        PE_SLOT = {1: ["project0"], 3: ["mean0"], 5: ["var0"], 9: ["up00"], 11: ["up01"], 12: ["down0"], 13: ["up10"],
                   14: ["up11"]}
        DVE_SLOT = {1: ["add_att"], 3: ["centre0"], 5: ["norm0"], 12: ["add_ffn0"]}
        ACT_SLOT = {3: ["square0"], 5: ["log0", "rstd0"], 6: ["affine0"], 9: ["gelu00"], 11: ["gelu01"],
                    13: ["gelu10"], 14: ["gelu11"]}
        MASK_AFTER = 13
        RSTD_AFTER, NORM_AFTER, AFFINE_AFTER, RES_AFTER = 5, 7, 7, 8
        K_AFTER, QV_AFTER, KEV_AFTER = 8, 14, 12

        NORM_BANKS = {0: acc, 2: ring[:, 1, :]}
        WIDE_BANKS = (ring[:, 0, :], ring[:, 1, :], acc[:], red[:])
        HALVES = [(b, t) for b in range(BATCH) for t in range(2)]

        def bank(b, t):
            return WIDE_BANKS[b][:, t * HALF:(t + 1) * HALF]

        def half(buf, b, t):
            return buf[:, b * SEQ + t * HALF:b * SEQ + (t + 1) * HALF]

        @block.sync
        def _(sp):
            for s in STARTED:
                sp.sem_inc(s, ONE)
            for dst, src in ((ident, ident_c), (mean_w, mean_c), (neg, neg_c), (cnt, cnt_c), (sel, sel_c),
                             (floor, floor_c), (lnf_s, lnf)):
                sp.dma_start(dst[:], src).then_inc(s_const, 16)
            sp.dma_start(s_c, c_t).then_inc(s_modw, 16)
            sp.dma_start(s_wmod, wmod.rearrange("p (m n) -> p m n", m=6)).then_inc(s_modw, 16)
            sp.dma_start(s_pe_view, pe_t).then_inc(s_modw, 16)
            for b in range(BATCH):
                sp.dma_start(x_all[:, b * SEQ:(b + 1) * SEQ], x_t[b]).then_inc(s_x[b], 16)
            for b in range(BATCH):
                sp.wait_ge(s_pe, ONE + b * 2 + 2)
                sp.dma_start(h_dram[b], x_all[:, b * SEQ:(b + 1) * SEQ]).then_inc(s_hst, 16)
            sp.wait_ge(s_hst, ONE + 16 * BATCH)
            with sp.Fori(0, LAYERS) as l:
                with sp.Fori(0, BATCH) as b:
                    it = l * BATCH + b
                    sp.wait_ge(s_vev, ONE + it)
                    sp.dma_start(wa_s[:], wa[bass.ds(l, 1)].rearrange("a p n -> p (a n)")).then_inc(s_wa, 16)
                    sp.wait_ge(s_hst, ONE + it * 16 + 16)
                    sp.wait_ge(s_res, ONE + it * 2)
                    sp.dma_start(h_in[:], h_dram[bass.ds(it, 1)].rearrange("a p n -> p (a n)")).then_inc(s_h, 16)
                    def load_keys(half, signal):
                        for h in range(HEADS):
                            p = slice(h * HD, (h + 1) * HD)
                            src = keys[p, :].rearrange("p (a l j) -> p a l j", a=2, l=LO)
                            sp.dma_start(diag[p, KEYS_AT[half], h * LO:(h + 1) * LO, :], src[:, half])\
                                .then_inc(signal, 16)

                    def load_values(half, signal):
                        for h in range(HEADS):
                            src = v_dram[h * HD:(h + 1) * HD, :].rearrange("d (l j) -> l d j", l=LO)
                            sp.dma_start(diag[h * LO:(h + 1) * LO, VALS_AT[half], h * HD:(h + 1) * HD, :],
                                         src[:, :, half * BLOCKS // 2:(half + 1) * BLOCKS // 2]).then_inc(signal, 16)

                    sp.wait_ge(s_zero, 3)
                    sp.wait_ge(s_full, ONE + it * SUNITS)
                    sp.wait_ge(s_kev, it + 1)
                    load_keys(0, s_kx0)
                    sp.wait_ge(s_vev, ONE + it + 1)
                    sp.wait_ge(s_vx1, ONE + it * 256)
                    sp.dma_start(v_dram, n_t[:]).then_inc(s_vst, 16)
                    sp.wait_ge(s_pv, ONE + it)
                    load_keys(1, s_kx1)
                    sp.wait_ge(s_vst, ONE + it * 16 + 16)
                    load_values(0, s_vx0)
                    sp.wait_ge(s_full, ONE + it * SUNITS + SUNITS)
                    load_values(1, s_vx1)
                    sp.wait_ge(s_lout, ONE + it * ITER_LN + PRE_LN)
                    sp.dma_start(wb_s[:], wb[bass.ds(l, 1)].rearrange("a p n -> p (a n)")).then_inc(s_wb, 16)
            sp.wait_ge(s_fin, ONE + 2 * ITERS - 1)
            for b in range(BATCH):
                sp.dma_start(x2[:, b * SEQ:(b + 1) * SEQ], x_t[b]).then_inc(s_x[b], 16)
            for dst, src in ((e_w1, we1), (e_w3, we3), (e_w2, we2), (e_ind, ind_c)):
                sp.dma_start(dst, src).then_inc(s_modw, 16)
            sp.dma_start(e_wg, w_gate).then_inc(s_modw, 16)
            for b in range(BATCH):
                sp.wait_ge(s_hst, ONE + 16 * (ITERS + b + 1))
                sp.dma_start(h_all[:, b * SEQ:(b + 1) * SEQ], h_dram[ITERS + b]).then_inc(s_h, 16)
            with sp.Fori(0, BATCH) as b:
                for t in range(2):
                    sp.wait_ge(s_od, ONE + b * 4 + 2 * t + 2)
                    sp.dma_start(out[bass.ds(b, 1), :, t * HALF:(t + 1) * HALF].rearrange("a p n -> p (a n)"),
                                 out_s[:, t, :]).then_inc(s_out, 16)
            sp.wait_ge(s_out, ONE + 16 * 2 * BATCH)

        @block.tensor
        def _(pe):
            mm = nc.tensor.matmul

            def ln_mean(n, src, t, banks=acc):
                cols = slice(t * HALF, (t + 1) * HALF)
                mm(banks[:, cols], mean_w[:], src[:, cols], start=True, stop=True).then_inc(s_lmean, 1)

            def ln_variance(n, t, banks=acc):
                cols = slice(t * HALF, (t + 1) * HALF)
                pe.wait_ge(s_lsq, n + 1)
                mm(banks[:, cols], mean_w[:], h_sq[:, cols], start=True, stop=True).then_inc(s_lvar, 1)

            def mean_all(src, b, t):
                mm(bank(b, t), mean_w[:], half(src, b, t), start=True, stop=True).then_inc(s_lmean, 1)

            def variance_all(n, squares):
                for k, (b, t) in enumerate(HALVES):
                    pe.wait_ge(s_lsq, n + k + 1)
                    mm(bank(b, t), mean_w[:], half(squares, b, t), start=True, stop=True).then_inc(s_lvar, 1)

            pe.wait_ge(s_modw, 48)
            pe.wait_ge(s_silu, 1)
            for m in range(6):
                last = mm(acc[:, m * BATCH:(m + 1) * BATCH], s_wmod[:, m, :], s_sig, start=True, stop=True)
            last.then_inc(s_modp, 1)
            pe.wait_ge(s_const, 16 * 7)
            pe.wait_ge(s_modv, 1)
            for b, t in HALVES:
                if t == 0:
                    pe.wait_ge(s_x[b], 16)
                mean_all(x_all, b, t)
            variance_all(0, x_sq)

            def tail(i, step):
                n = i * ITER_LN + PRE_LN
                name, arg = step[:-1], int(step[-1])
                if name == "project":
                    pe.wait_ge(s_wb, i * 16 + 16)
                    pe.wait_ge(s_fin, ONE + i * 2 + 2)
                    for t in range(2):
                        mm(acc[:, t * HALF:(t + 1) * HALF], wo, att[:, t * HALF:(t + 1) * HALF],
                           start=True, stop=True).then_inc(s_op, 1)
                elif name == "mean":
                    for t in range(2):
                        pe.wait_ge(s_lin, i * ITER_LN + arg + t + 1)
                        ln_mean(n + arg + t, res, t, NORM_BANKS[arg])
                elif name == "var":
                    for t in range(2):
                        ln_variance(n + arg + t, t, NORM_BANKS[arg])
                elif name[:2] == "up":
                    t, p = int(step[2]), arg
                    pe.wait_ge(s_lout, ONE + n + 2)
                    if t or p:
                        pe.wait_ge(s_gelu, i * 2 * FCH + FCH * t + 2 * p)
                    if t and not p:
                        pe.wait_ge(s_lin, i * ITER_LN + 3)
                    for c in range(2):
                        mm(acc[:, c * HALF:(c + 1) * HALF], w1[:, 2 * p + c, :], att[:, t * HALF:(t + 1) * HALF],
                           start=True, stop=True).then_inc(s_w1, 1)
                else:
                    t = arg
                    pe.wait_ge(s_gelu, i * 2 * FCH + FCH * (t + 1))
                    for c in range(FCH):
                        last = mm(acc[:, t * HALF:(t + 1) * HALF], w2[:, c, :], gl[:, c, :],
                                  start=(c == 0), stop=(c == FCH - 1))
                    last.then_inc(s_w2, 1)

            def project(n, name, dst):
                w, signal = {"q": (0, s_qpr), "k": (1, s_kpr), "v": (2, s_vpr)}[name]
                if name == "k":
                    pe.wait_ge(s_wa, n * 16 + 16)
                    pe.wait_ge(s_h, n * 16 + 16)
                for t in range(2):
                    last = mm(dst[:, t * HALF:(t + 1) * HALF], wa_s[:, w * D:(w + 1) * D],
                              h_in[:, t * HALF:(t + 1) * HALF], start=True, stop=True)
                last.then_inc(signal, 1)

            def spread(i):
                pe.wait_ge(s_rec, i * 3 + 3)
                for cols in TILE_COLS:
                    last = nc.tensor.transpose(red[:, cols], q_t[:, cols], ident[:])
                last.then_inc(s_denb, 1)

            def iteration(it, with_tail=True, with_next=True):
                pe.wait_ge(s_qev, it + 1)
                pe.wait_ge(s_kx0, it * 256 + 256)
                for u in range(SUNITS):
                    if u == 1:
                        pe.wait_ge(s_vev, ONE + it + 1)
                    elif u >= 2:
                        pe.wait_ge(s_free, ONE + it * SUNITS + u - 1)
                    dst = ring[:, u % 2, :]
                    for j, col, nj in ORDER[u]:
                        if j == FIRST_HIGH:
                            pe.wait_ge(s_kx1, it * 256 + 256)
                        jh, jr = divmod(j, BLOCKS // 2)
                        for top in ((0, 1) if nj > HALF else (None,)):
                            for off, n, rs in pieces(j, nj, fixed_top=top):
                                c = col - u * UNIT + off
                                last = mm(view_block(dst[:, c:c + n], rs), diag[:, KEYS_AT[jh], :, jr],
                                          view_queries(k_t[:], rs),
                                          start=True, stop=True)
                        if j == ORDER[u][-1][0]:
                            last.then_inc(s_full, 1)
                    if with_tail:
                        if u == SPREAD_AFTER:
                            spread(it - 1)
                        for step in PE_SLOT.get(u, ()):
                            tail(it - 1, step)
                if with_tail:
                    tail(it - 1, "down1")
                pe.wait_ge(s_free, ONE + it * SUNITS + SUNITS)
                pe.wait_ge(s_max, it * MAX_STEPS + MAX_STEPS)
                for cols in TILE_COLS:
                    last = nc.tensor.transpose(ring[:, 0, cols], q_t[:, cols], ident[:])
                last.then_inc(s_rtr, 1)
                if with_tail:
                    tail(it - 1, "mean2")
                pe.wait_ge(s_m, it * 4 + 4)
                for cols in TILE_COLS:
                    last = nc.tensor.transpose(red[:, cols], q_t[:, cols], ident[:])
                last.then_inc(s_mb, 1)
                for cols in TILE_COLS:
                    last = nc.tensor.transpose(ring[:, 0, cols], q_t[:, cols], ident[:])
                last.then_inc(s_mbe, 1)
                if with_tail:
                    tail(it - 1, "var2")
                pe.wait_ge(s_vx0, it * 256 + 256)
                for u in range(SUNITS):
                    pe.wait_ge(s_exp, it * SUNITS + u + 1)
                    for j, col, nj in ORDER[u]:
                        if j == FIRST_HIGH:
                            pe.wait_ge(s_vx1, ONE + it * 256 + 256)
                        jh, jr = divmod(j, BLOCKS // 2)
                        vals = diag[:, VALS_AT[jh], :, jr]
                        for top in (0, 1):
                            for off, n, rs in pieces(j, nj, fixed_top=top):
                                last = mm(view_queries(acc[:], rs), vals,
                                          view_block(score[:, col + off:col + off + n], rs),
                                          start=(j == 0), stop=(j == LAST_HIGH or (j == LAST_LOW and top == 1)),
                                          skip_group_check=True)
                    if u == SUNITS - 1:
                        last.then_inc(s_pv, 1)
                    if with_next and u == K_AFTER:
                        if with_tail:
                            pe.wait_ge(s_lin, it * ITER_LN)
                        project(it + 1, "k", ring[:, 0, :])
                    if with_next and u == QV_AFTER:
                        pe.wait_ge(s_kev, it + 2)
                        project(it + 1, "q", ring[:, 0, :])
                        if with_tail:
                            pe.wait_ge(s_lnorm, it * ITER_LN + PRE_LN)
                        project(it + 1, "v", ring[:, 1, :])
                pe.wait_ge(s_den, it * len(LOWP) + len(LOWP))
                pe.wait_ge(s_dend, it * (len(HIGHP) + 1) + len(HIGHP) + 1)
                for c, cols in enumerate(TILE_COLS):
                    last = mm(red[:, c * HEADS:(c + 1) * HEADS], q_t[:, cols], sel[:], start=True, stop=True)
                last.then_inc(s_dtok, 1)

            project(0, "k", ring[:, 0, :])
            pe.wait_ge(s_kev, 1)
            project(0, "q", ring[:, 0, :])
            project(0, "v", ring[:, 1, :])
            iteration(0, with_tail=False)
            with pe.Fori(1, ITERS - 1) as it:
                iteration(it)
            iteration(ITERS - 1, with_next=False)
            spread(ITERS - 1)
            for u in range(SUNITS):
                for step in PE_SLOT.get(u, ()):
                    tail(ITERS - 1, step)
            for step in ("down1", "mean2", "var2"):
                tail(ITERS - 1, step)

            base = PRE_LN + ITERS * ITER_LN
            pe.wait_ge(s_h, (ITERS + BATCH) * 16)
            pe.wait_ge(s_lnorm, base)
            for b, t in HALVES:
                mean_all(h_all, b, t)
            variance_all(base, h_nrm)
            for k, (b, t) in enumerate(HALVES):
                pe.wait_ge(s_x2, ONE + k + 1)
                mean_all(x2, b, t)
            variance_all(base + 2 * BATCH, h_nrm)
            pe.wait_ge(s_modw, 48 + 80)
            for c in range(TILES):
                if c % 4 == 0:
                    pe.wait_ge(s_lout, ONE + base + 2 * BATCH + c // 4 + 1)
                if c == 0:
                    pe.wait_ge(s_lnorm, base + 4 * BATCH)
                last = mm(acc[:, c * EXPERTS:(c + 1) * EXPERTS], hm[:, c * 128:(c + 1) * 128], e_wg,
                          start=True, stop=True)
            last.then_inc(s_gate, 1)
            pe.wait_ge(s_gv, GATE_STEPS)
            for r in range(4):
                if r >= 2:
                    pe.wait_ge(s_ctc, r - 1)
                for c in range(8):
                    k = r * 8 + c
                    last = nc.tensor.transpose(ring[0:PARTS * EXPERTS, r % 2, c * 128:(c + 1) * 128],
                                               m_parts[:, k].rearrange("p a e -> p (a e)"), ident[:])
                last.then_inc(s_ctp, 1)
            pe.wait_ge(s_ctc, 5)
            with pe.Fori(0, BATCH) as b:
                for t in range(2):
                    for c in range(MCH + 1):
                        if c < MCH:
                            n = 2 * MCH * b + t * MCH + c
                            q = (t * MCH + c) % 2
                            rhs = hm[:, bass.ds(b * SEQ + t * HALF, HALF)]
                            pe.wait_ge(s_act, ONE + (n - 1 if t or c else n))
                            mm(ring[:, q, 0:HALF], e_w1[:, c, :], rhs, start=True, stop=True)
                            mm(ring[:, q, HALF:UNIT], e_w3[:, c, :], rhs, start=True, stop=True).then_inc(s_gu, 1)
                            if c < MCH - 1:
                                mm(red[:, q * HALF:(q + 1) * HALF], e_ind_bf[:, c, :],
                                   comb_t[:, bass.ds(b * SEQ + t * HALF, HALF)], start=True, stop=True)\
                                    .then_inc(s_cb, 1)
                        if c >= 1:
                            n = 2 * MCH * b + t * MCH + c - 1
                            pe.wait_ge(s_act, ONE + n + 1)
                            if c == 1:
                                pe.wait_ge(s_od, ONE + b * 4)
                            last = mm(acc[:, t * HALF:(t + 1) * HALF], e_w2[:, c - 1, :],
                                      m_z[:, (t * MCH + c - 1) % 2, :], start=(c == 1), stop=(c == MCH))
                    last.then_inc(s_eo, 1)

        @block.scalar
        def _(act):
            A = nc.scalar.activation

            def ln_square(n, t):
                cols = slice(t * HALF, (t + 1) * HALF)
                act.wait_ge(s_lcen, n + 1)
                A(h_sq[:, cols], res[:, cols], ACT.Square).then_inc(s_lsq, 1)

            def ln_log(n, banks=acc):
                for t in range(2):
                    act.wait_ge(s_lvar, n + t + 1)
                    A(banks[:, t * HALF:(t + 1) * HALF], banks[:, t * HALF:(t + 1) * HALF], ACT.Ln, bias=eps[:])\
                        .then_inc(s_lln, 1)

            def ln_rstd(n, banks=acc):
                for t in range(2):
                    act.wait_ge(s_lln, n + t + 1)
                    A(banks[:, t * HALF:(t + 1) * HALF], banks[:, t * HALF:(t + 1) * HALF], ACT.Exp, scale=-0.5)\
                        .then_inc(s_lstd, 1)

            def ln_affine(n, t, dst, g, beta):
                cols = slice(t * HALF, (t + 1) * HALF)
                act.wait_ge(s_lnorm, n + 1)
                A(dst[:, cols] if not isinstance(dst, list) else dst[t], h_sq[:, cols], ACT.Identity,
                  scale=g, bias=beta).then_inc(s_lout, 1)

            def norm_all(n, centred, normed, dst, g, beta):
                for k, (b, t) in enumerate(HALVES):
                    act.wait_ge(s_lcen, n + k + 1)
                    A(half(normed, b, t), half(centred, b, t), ACT.Square).then_inc(s_lsq, 1)
                for k, (b, t) in enumerate(HALVES):
                    act.wait_ge(s_lvar, n + k + 1)
                    A(bank(b, t), bank(b, t), ACT.Ln, bias=eps[:]).then_inc(s_lln, 1)
                for k, (b, t) in enumerate(HALVES):
                    act.wait_ge(s_lln, n + k + 1)
                    A(bank(b, t), bank(b, t), ACT.Exp, scale=-0.5).then_inc(s_lstd, 1)
                for k, (b, t) in enumerate(HALVES):
                    act.wait_ge(s_lnorm, n + k + 1)
                    A(half(dst, b, t), half(normed, b, t), ACT.Identity, scale=g(b), bias=beta(b)).then_inc(s_lout, 1)

            act.wait_ge(s_modw, 48)
            A(s_sgn[:, 0:BATCH], s_c, ACT.Exp, scale=-1.0).then_inc(s_silu_e, 1)
            act.wait_ge(s_modv, MOD_STEPS)
            act.wait_ge(s_eps, 2)
            act.wait_ge(s_const, 16 * 7)
            norm_all(0, x_cen, x_sq, x_all, lambda b: mod[:, 1, b:b + 1], lambda b: mod[:, 0, b:b + 1])

            def tail(i, step, keys_loaded=256 * ITERS):
                n = i * ITER_LN + PRE_LN
                arg = int(step[-1])
                if step.startswith("square"):
                    for t in range(2):
                        ln_square(n + arg + t, t)
                elif step.startswith("log"):
                    ln_log(n + arg, NORM_BANKS[arg])
                elif step.startswith("rstd"):
                    ln_rstd(n + arg, NORM_BANKS[arg])
                elif step.startswith("gelu"):
                    t, p = int(step[4]), arg
                    if t and not p:
                        act.wait_ge(s_w2, i * 2 + 1)
                    if not t and not p:
                        act.wait_ge(s_lout, ONE + n + 2)
                    if not t and p:
                        act.wait_ge(s_kx0, keys_loaded)
                        act.wait_ge(s_kx1, keys_loaded)
                    for c in range(2):
                        k = 2 * p + c
                        act.wait_ge(s_w1, i * 2 * FCH + FCH * t + k + 1)
                        A(gl[:, k, :], acc[:, c * HALF:(c + 1) * HALF], ACT.Gelu, bias=b1[k]).then_inc(s_gelu, 1)
                else:
                    g, beta = (g2, be2) if arg else (g1, be1)
                    for t in range(2):
                        ln_affine(n + arg + t, t, att, g, beta)
                    if arg:
                        act.wait_ge(s_lout, ONE + n + ITER_LN)
                        act.dma_start(h_dram[bass.ds(i + BATCH, 1)].rearrange("a p n -> p (a n)"), att[:])\
                            .then_inc(s_hst, 16)

            def evacuate(n, name):
                if name == "k":
                    act.wait_ge(s_kpr, n + 1)
                    A(keys.rearrange("p (a l j) -> p a j l", a=2, l=LO),
                      ring[:, 0, :].rearrange("p (a j l) -> p a j l", a=2, l=LO), ACT.Identity, bias=bk).then_inc(s_kev, 1)
                elif name == "v":
                    act.wait_ge(s_vpr, n + 1)
                    A(n_t[:].rearrange("p (l j) -> p j l", l=LO),
                      ring[:, 1, :].rearrange("p (j l) -> p j l", l=LO), ACT.Identity, bias=bv).then_inc(s_vev, 1)
                else:
                    act.wait_ge(s_qpr, n + 1)
                    A(k_t[:], ring[:, 0, :], ACT.Identity, bias=bq).then_inc(s_qev, 1)

            def iteration(it, with_tail=True, with_next=True):
                for u in range(SUNITS):
                    act.wait_ge(s_full, ONE + it * SUNITS + u + 1)
                    for a, z in unit_spans(u):
                        last = A(score[:, u * UNIT + a:u * UNIT + z], ring[:, u % 2, a:z], ACT.Copy,
                                 scale=SCALE)
                    last.then_inc(s_free, 1)
                    if with_tail:
                        for step in ACT_SLOT.get(u, ()):
                            tail(it - 1, step, it * 256 + 256)
                act.wait_ge(s_m, it * 4 + 3)
                A(e_tok[:], m_tok[:], ACT.Exp, scale=-1.0).then_inc(s_etok, 1)
                if with_tail:
                    tail(it - 1, "square2")
                act.wait_ge(s_mbe, it + 1)
                act.wait_ge(s_z, it * 11 + 11)
                A(n_t[:], ring[:, 0, :], ACT.Exp, scale=-1.0).then_inc(s_e0, 1)
                for u in range(SUNITS):
                    act.wait_ge(s_shift, it * SUNITS + u + 1)
                    for a, z in unit_spans(u):
                        last = A(score[:, u * UNIT + a:u * UNIT + z], score[:, u * UNIT + a:u * UNIT + z], ACT.Exp)
                    last.then_inc(s_exp, 1)
                    if with_tail and u == RSTD_AFTER:
                        tail(it - 1, "log2")
                        tail(it - 1, "rstd2")
                    if with_tail and u == AFFINE_AFTER:
                        tail(it - 1, "affine2")
                    if u == RES_AFTER:
                        if with_tail:
                            act.wait_ge(s_lnorm, it * ITER_LN + PRE_LN)
                        A(res[:], h_in[:], ACT.Copy).then_inc(s_res, 2)
                    if with_next and u == KEV_AFTER:
                        if with_tail:
                            act.wait_ge(s_w2, it * 2)
                        evacuate(it + 1, "k")
                if with_next:
                    act.wait_ge(s_ec, it + 1)
                    evacuate(it + 1, "q")
                    act.wait_ge(s_fin, ONE + it * 2 + 1)
                    evacuate(it + 1, "v")

            for name in ("k", "q", "v"):
                evacuate(0, name)
            iteration(0, with_tail=False)
            with act.Fori(1, ITERS - 1) as it:
                iteration(it)
            iteration(ITERS - 1, with_next=False)
            for u in range(SUNITS):
                for step in ACT_SLOT.get(u, ()):
                    tail(ITERS - 1, step)
            for step in ("square2", "log2", "rstd2", "affine2"):
                tail(ITERS - 1, step)

            base = PRE_LN + ITERS * ITER_LN
            norm_all(base, h_cen, h_nrm, h_all, lambda b: lnf_s[:, 0:1], lambda b: lnf_s[:, 1:2])
            norm_all(base + 2 * BATCH, h_cen, h_nrm, hm, lambda b: mod[:, 4, b:b + 1], lambda b: mod[:, 3, b:b + 1])
            act.wait_ge(s_gate, 1)
            A(m_a, acc[:, 0:512], ACT.Exp, scale=-1.0).then_inc(s_gexp, 1)
            for r in range(4):
                act.wait_ge(s_ctp, r + 1)
                A(comb_t[:, r * SEQ:(r + 1) * SEQ], ring[0:PARTS * EXPERTS, r % 2, :], ACT.Copy).then_inc(s_ctc, 1)
            A(e_ind_bf, e_ind, ACT.Copy).then_inc(s_ctc, 1)
            with act.Fori(0, BATCH) as b:
                act.wait_ge(s_od, ONE + b * 4)
                A(cur[:], mod[:, :, bass.ds(b, 1)].rearrange("p m a -> p (m a)"), ACT.Copy).then_inc(s_cur, 1)
                for t in range(2):
                    for c in range(MCH):
                        n = 2 * MCH * b + t * MCH + c
                        q = (t * MCH + c) % 2
                        act.wait_ge(s_gu, n + 1)
                        act.wait_ge(s_act, ONE + (n - 1 if t or c else n))
                        A(m_sg[:, q, :], ring[:, q, 0:HALF], ACT.Silu).then_inc(s_sg, 1)

        @block.vector
        def _(dve):
            V = nc.vector

            def ln_centre(n, src, t, banks=acc):
                cols = slice(t * HALF, (t + 1) * HALF)
                dve.wait_ge(s_lmean, n + 1)
                V.tensor_tensor(res[:, cols], src[:, cols], banks[:, cols], ALU.subtract).then_inc(s_lcen, 1)

            def ln_norm(n, t, banks=acc):
                cols = slice(t * HALF, (t + 1) * HALF)
                dve.wait_ge(s_lstd, n + 1)
                V.tensor_tensor(h_sq[:, cols], banks[:, cols], res[:, cols], ALU.mult).then_inc(s_lnorm, 1)

            def centre_all(n, src, centred):
                for k, (b, t) in enumerate(HALVES):
                    dve.wait_ge(s_lmean, n + k + 1)
                    V.tensor_tensor(half(centred, b, t), half(src, b, t), bank(b, t), ALU.subtract).then_inc(s_lcen, 1)

            def scale_all(n, centred, normed):
                for k, (b, t) in enumerate(HALVES):
                    dve.wait_ge(s_lstd, n + k + 1)
                    V.tensor_tensor(half(normed, b, t), bank(b, t), half(centred, b, t), ALU.mult).then_inc(s_lnorm, 1)

            V.memset(eps[:], EPS).then_inc(s_eps, 1)
            V.memset(one[:], 1.0).then_inc(s_eps, 1)
            mv = chain(dve, s_dv)
            dve.wait_ge(s_silu_e, 1)
            mv(V.tensor_scalar(s_sgn[:, 0:BATCH], s_sgn[:, 0:BATCH], 1.0, None, ALU.add))
            mv(V.reciprocal(s_sgn[:, 0:BATCH], s_sgn[:, 0:BATCH]))
            V.tensor_tensor(s_sig, s_c, s_sgn[:, 0:BATCH], ALU.mult).then_inc(s_silu, 1)
            dve.wait_ge(s_modp, 1)
            V.tensor_copy(mod[:], acc[:, 0:6 * BATCH].rearrange("p (m b) -> p m b", m=6)).then_inc(s_modv, 1)
            dve.wait_ge(s_modv, 1)
            dve.wait_ge(s_silu, 1)
            for m in (1, 4):
                V.tensor_scalar(mod[:, m, :], mod[:, m, :], 1.0, None, ALU.add).then_inc(s_modv, 1)
            for m in (2, 5):
                mv(V.tensor_scalar(s_sgn[:, 0:BATCH], mod[:, m, :], 0.0, 2.0, ALU.is_ge, ALU.mult))
                mv(V.tensor_scalar(s_sgn[:, BATCH:2 * BATCH], mod[:, m, :], -1.0, 0.25, ALU.mult, ALU.max))
                mv(V.tensor_tensor(s_sgn[:, BATCH:2 * BATCH], s_sgn[:, BATCH:2 * BATCH], mod[:, m, :], ALU.max))
                mv(V.tensor_scalar(s_sgn[:, 0:BATCH], s_sgn[:, 0:BATCH], -1.0, None, ALU.add))
                mv(V.tensor_tensor(mod[:, m, :], s_sgn[:, 0:BATCH], s_sgn[:, BATCH:2 * BATCH], ALU.mult)) \
                    if m == 2 else V.tensor_tensor(mod[:, m, :], s_sgn[:, 0:BATCH], s_sgn[:, BATCH:2 * BATCH],
                                                   ALU.mult).then_inc(s_modv, 1)
            assert MOD_STEPS == 4
            dve.wait_ge(s_modw, 48)
            centre_all(0, x_all, x_cen)
            scale_all(0, x_cen, x_sq)
            for k, (b, t) in enumerate(HALVES):
                dve.wait_ge(s_lout, ONE + k + 1)
                V.tensor_tensor(half(x_all, b, t), half(x_all, b, t), s_pe_view[:, t * HALF:(t + 1) * HALF], ALU.add)\
                    .then_inc(s_pe, 1)

            def tail(i, step):
                n = i * ITER_LN + PRE_LN
                if step == "add_att":
                    for t in range(2):
                        cols = slice(t * HALF, (t + 1) * HALF)
                        dve.wait_ge(s_op, i * 2 + t + 1)
                        V.scalar_tensor_tensor(out=res[:, cols], in0=acc[:, cols], scalar=bo, in1=res[:, cols],
                                               op0=ALU.add, op1=ALU.add).then_inc(s_lin, 1)
                elif step.startswith("add_ffn"):
                    t = int(step[-1])
                    cols = slice(t * HALF, (t + 1) * HALF)
                    dve.wait_ge(s_w2, i * 2 + t + 1)
                    V.scalar_tensor_tensor(out=res[:, cols], in0=acc[:, t * HALF:(t + 1) * HALF], scalar=b2, in1=att[:, cols],
                                           op0=ALU.add, op1=ALU.add).then_inc(s_lin, 1)
                else:
                    arg = int(step[-1])
                    for t in range(2):
                        if step.startswith("centre"):
                            ln_centre(n + arg + t, res, t, NORM_BANKS[arg])
                        else:
                            ln_norm(n + arg + t, t, NORM_BANKS[arg])

            def iteration(it, with_tail=True, with_next=True):
                base = it * MAX_STEPS
                neg_b = neg[:].unsqueeze(1).broadcast_to([128, BLOCKS, LO])

                def mask_pairs(a, z):
                    V.tensor_tensor(q_t[:, a:z].rearrange("p (i l) -> p i l", l=LO),
                                    red[:, a:z].rearrange("p (i l) -> p i l", l=LO), neg_b[:, 0:(z - a) // LO],
                                    ALU.add).then_inc(s_max, 1)

                steps, newest = 0, {}
                for k, (u, col, off, n, rs) in enumerate(MAXP):
                    if k == 0 or MAXP[k - 1][0] != u:
                        dve.wait_ge(s_free, ONE + it * SUNITS + u + 1)
                    s = view_block(score[:, col + off:col + off + n], rs)
                    high = k - (NMAX - len(HIGHP))
                    side = "q_t" if high > 0 and high % 2 else "red"
                    r = view_queries(q_t[:] if side == "q_t" else red[:], rs)
                    if k == 0:
                        if with_tail:
                            dve.wait_ge(s_fin, ONE + it * 2)
                        V.tensor_copy(r, s).then_inc(s_max, 1)
                    else:
                        dve.wait_ge(s_max, base + newest[side])
                        V.tensor_tensor(r, r, s, ALU.max).then_inc(s_max, 1)
                    steps += 1
                    newest[side] = steps
                    if high == 0:
                        V.tensor_copy(view_queries(q_t[:], rs), s).then_inc(s_max, 1)
                        steps += 1
                        newest["q_t"] = steps
                    if with_tail and (k == NMAX - 1 or MAXP[k + 1][0] != u):
                        for step in DVE_SLOT.get(u, ()):
                            tail(it - 1, step)
                    if u == MASK_AFTER and MAXP[k + 1][0] != u:
                        dve.wait_ge(s_max, base + newest["red"])
                        mask_pairs(HALF, SEQ)
                        steps += 1
                dve.wait_ge(s_max, base + steps)
                V.tensor_tensor(red[:, 0:HALF], red[:, 0:HALF], q_t[:, 0:HALF], ALU.max).then_inc(s_max, 1)
                dve.wait_ge(s_max, base + steps + 1)
                mask_pairs(0, HALF)
                assert steps + 2 == MAX_STEPS
                if with_tail:
                    tail(it - 1, "add_ffn1")
                dve.wait_ge(s_rtr, it + 1)
                V.tensor_reduce(m_tok[:], ring[:, 0, :].rearrange("p (g l) -> p g l", l=LO), AX_X, ALU.max)\
                    .then_inc(s_m, 1)
                dve.wait_ge(s_m, it * 4 + 1)
                V.tensor_scalar(m_tok[:, 0:HEADS], m_tok[:, 0:HEADS], floor[:], None, ALU.max).then_inc(s_m, 1)
                V.tensor_scalar(m_tok[:, HEADS:], m_tok[:, HEADS:], 0.0, None, ALU.max).then_inc(s_m, 1)
                dve.wait_ge(s_m, it * 4 + 3)
                lanes = q_t[:].rearrange("p (g l) -> p g l", l=LO)
                V.tensor_copy(lanes, m_tok[:].unsqueeze(2).broadcast_to([128, BLOCKS, LO])).then_inc(s_m, 1)
                dve.wait_ge(s_etok, it * 2 + 1)
                V.tensor_tensor(e_tok[:].rearrange("p (c h) -> p c h", h=HEADS),
                                e_tok[:].rearrange("p (c h) -> p c h", h=HEADS),
                                cnt[:].unsqueeze(2).broadcast_to([128, SEQ // 128, HEADS]), ALU.mult)\
                    .then_inc(s_etok, 1)
                if with_tail:
                    tail(it - 1, "centre2")
                dve.wait_ge(s_mb, it + 1)
                red_v = red[:].rearrange("p (i l) -> p i l", l=LO)
                V.scalar_tensor_tensor(out=red_v, in0=red_v, scalar=-1.0, in1=neg_b, op0=ALU.mult, op1=ALU.add)\
                    .then_inc(s_b, 1)
                dve.wait_ge(s_b, it + 1)
                for k, (u, col, off, n, rs) in enumerate(MAXP):
                    s = view_block(score[:, col + off:col + off + n], rs)
                    last = V.tensor_tensor(s, view_queries(red[:], rs), s, ALU.add)
                    if k == NMAX - 1 or MAXP[k + 1][0] != u:
                        last.then_inc(s_shift, 1)
                        if with_tail and u == NORM_AFTER:
                            tail(it - 1, "norm2")
                base = it * (len(HIGHP) + 1)
                dve.wait_ge(s_shift, it * SUNITS + SUNITS)
                for k, (u, col, off, n, rs) in enumerate(HIGHP):
                    if k == 0 or HIGHP[k - 1][0] != u:
                        dve.wait_ge(s_exp, it * SUNITS + u + 1)
                    if k:
                        dve.wait_ge(s_dend, base + k)
                    s = view_block(score[:, col + off:col + off + n], rs)
                    r = view_queries(red[:], rs)
                    if k == 0:
                        V.tensor_copy(r, s).then_inc(s_dend, 1)
                    else:
                        V.tensor_tensor(r, r, s, ALU.add).then_inc(s_dend, 1)
                dve.wait_ge(s_dend, base + len(HIGHP))
                dve.wait_ge(s_den, it * len(LOWP) + len(LOWP))
                V.tensor_tensor(q_t[:, 0:HALF], red[:, 0:HALF], q_t[:, 0:HALF], ALU.add).then_inc(s_dend, 1)
                dve.wait_ge(s_pv, ONE + it + 1)
                dve.wait_ge(s_ec, it + 1)
                dve.wait_ge(s_hst, ONE + it * 16 + 16 * BATCH)
                V.tensor_tensor(att[:], acc[:], n_t[:], ALU.add).then_inc(s_fin, 1)
                dve.wait_ge(s_dtok, it + 1)
                V.tensor_tensor(m_tok[:], red[:, 0:BLOCKS], e_tok[:], ALU.add).then_inc(s_rec, 1)
                dve.wait_ge(s_rec, it * 3 + 1)
                V.reciprocal(m_tok[:], m_tok[:]).then_inc(s_rec, 1)
                dve.wait_ge(s_rec, it * 3 + 2)
                V.tensor_copy(lanes, m_tok[:].unsqueeze(2).broadcast_to([128, BLOCKS, LO])).then_inc(s_rec, 1)
                dve.wait_ge(s_denb, it + 1)
                dve.wait_ge(s_fin, ONE + it * 2 + 1)
                V.tensor_tensor(att[:], red[:], att[:], ALU.mult).then_inc(s_fin, 1)

            iteration(0, with_tail=False)
            with dve.Fori(1, ITERS - 1) as it:
                iteration(it)
            iteration(ITERS - 1, with_next=False)
            for u in range(SUNITS):
                for step in DVE_SLOT.get(u, ()):
                    tail(ITERS - 1, step)
            for step in ("add_ffn1", "centre2", "norm2"):
                tail(ITERS - 1, step)

            base = PRE_LN + ITERS * ITER_LN
            centre_all(base, h_all, h_cen)
            scale_all(base, h_cen, h_nrm)
            for k, (b, t) in enumerate(HALVES):
                if t == 0:
                    dve.wait_ge(s_x[b], 32)
                dve.wait_ge(s_lout, ONE + base + k + 1)
                V.scalar_tensor_tensor(out=half(x2, b, t), in0=half(h_all, b, t), scalar=mod[:, 2, b:b + 1],
                                       in1=half(x2, b, t), op0=ALU.mult, op1=ALU.add).then_inc(s_x2, 1)
            centre_all(base + 2 * BATCH, x2, h_cen)
            scale_all(base + 2 * BATCH, h_cen, h_nrm)

            g = chain(dve, s_dv, start=mv.count[0])
            dve.wait_ge(s_gexp, 1)
            dve.wait_ge(s_modw, 48 + 80)
            g(V.tensor_scalar(m_g, m_a, 1.0, None, ALU.add))
            g(V.reciprocal(m_g, m_g))
            s4 = m_g.rearrange("p (q e) -> p q e", e=4)
            hi1, lo1, hi2, lo2 = m_t
            g(V.tensor_tensor(hi1, s4[:, :, 0], s4[:, :, 1], ALU.max))
            g(V.tensor_tensor(lo1, s4[:, :, 0], s4[:, :, 1], ALU.min))
            g(V.tensor_tensor(hi2, s4[:, :, 2], s4[:, :, 3], ALU.max))
            g(V.tensor_tensor(lo2, s4[:, :, 2], s4[:, :, 3], ALU.min))
            g(V.tensor_tensor(m_gs, hi1, hi2, ALU.max))
            g(V.tensor_tensor(hi1, hi1, hi2, ALU.min))
            g(V.tensor_tensor(lo1, lo1, lo2, ALU.max))
            g(V.tensor_tensor(hi1, hi1, lo1, ALU.max))
            g(V.tensor_tensor(m_gs, m_gs, hi1, ALU.add))

            def ranks(dst, val, width):
                n = TILES * width * width
                v = val.rearrange("p (t e) -> p t e", e=width)
                c = m_c1[:, 0:n].rearrange("p (t e o) -> p t e o", t=TILES, e=width)
                for e in range(width):
                    own = v[:, :, e:e + 1]
                    if e:
                        V.tensor_tensor(c[:, :, e, 0:e], v[:, :, 0:e], own.broadcast_to([128, TILES, e]), ALU.is_ge)\
                            .then_inc(s_rank, 1)
                    V.tensor_tensor(c[:, :, e, e:], v[:, :, e:], own.broadcast_to([128, TILES, width - e]), ALU.is_gt)\
                        .then_inc(s_rank, 1)
                ranked[0] += 2 * width - 1
                dve.wait_ge(s_rank, ranked[0])
                g(V.tensor_reduce(dst, m_c1[:, 0:n].rearrange("p (q o) -> p q o", o=width), AX_X, ALU.add))

            ranked = [0]
            ranks(m_al, m_gs, GROUPS)
            g(V.tensor_scalar(m_al, m_al, 1.5, None, ALU.is_lt))
            al = m_al.unsqueeze(2).broadcast_to([128, TILES * GROUPS, 4])
            m_b4 = m_b.rearrange("p (q e) -> p q e", e=4)
            g(V.tensor_tensor(m_b4, s4, al, ALU.mult))
            g(V.tensor_scalar(m_al, m_al, -1.0, None, ALU.add))
            g(V.tensor_tensor(m_b4, m_b4, al, ALU.add))
            ranks(m_a, m_b, EXPERTS)
            g(V.tensor_scalar(m_a, m_a, 3.5, None, ALU.is_lt))
            g(V.tensor_tensor(m_a, m_a, m_g, ALU.mult))
            a3 = m_a.rearrange("p (t e) -> p t e", e=EXPERTS)
            g(V.tensor_reduce(m_t[0][:, 0:TILES], a3, AX_X, ALU.add))
            g(V.tensor_scalar(m_t[0][:, 0:TILES], m_t[0][:, 0:TILES], 1e-6, None, ALU.add))
            g(V.reciprocal(m_t[0][:, 0:TILES], m_t[0][:, 0:TILES]))
            g(V.tensor_tensor(a3, a3, m_t[0][:, 0:TILES].unsqueeze(2).broadcast_to([128, TILES, EXPERTS]), ALU.mult))
            for part in range(PARTS):
                g(V.tensor_copy(m_bf, a3))
                copied = V.tensor_copy(m_parts[:, :, part, :], m_bf)
                if part < PARTS - 1:
                    g(copied)
                    g(V.tensor_tensor(a3, a3, m_parts[:, :, part, :], ALU.subtract))
                else:
                    copied.then_inc(s_gv, GATE_STEPS)
            with dve.Fori(0, BATCH) as b:
                dve.wait_ge(s_cur, b + 1)
                for t in range(2):
                    for c in range(MCH):
                        n = 2 * MCH * b + t * MCH + c
                        q = (t * MCH + c) % 2
                        dve.wait_ge(s_sg, n + 1)
                        if c < MCH - 1:
                            V.tensor_tensor(m_y[:, q, :], m_sg[:, q, :], ring[:, q, HALF:UNIT], ALU.mult)\
                                .then_inc(s_hvs, 1)
                            steps = 2 * (MCH - 1) * b + t * (MCH - 1) + c + 1
                            dve.wait_ge(s_hvs, steps)
                            dve.wait_ge(s_cb, steps)
                            V.tensor_tensor(m_z[:, q, :], m_y[:, q, :], red[:, q * HALF:(q + 1) * HALF], ALU.mult)\
                                .then_inc(s_act, 1)
                        else:
                            V.tensor_tensor(m_z[:, q, :], m_sg[:, q, :], ring[:, q, HALF:UNIT], ALU.mult)\
                                .then_inc(s_act, 1)
                    cols = slice(t * HALF, (t + 1) * HALF)
                    dve.wait_ge(s_eo, b * 2 + t + 1)
                    dve.wait_ge(s_out, ONE + b * 32)
                    V.tensor_scalar(out_s[:, t, :], acc[:, cols], cur[:, 5:6], None, ALU.mult).then_inc(s_od, 1)
                    dve.wait_ge(s_od, ONE + b * 4 + 2 * t + 1)
                    V.tensor_tensor(out_s[:, t, :], out_s[:, t, :], x2[:, bass.ds(b * SEQ + t * HALF, HALF)],
                                    ALU.add).then_inc(s_od, 1)

        @block.gpsimd
        def _(pool):
            P = nc.gpsimd
            for a in (1, 0, 2):
                P.memset(diag[:, a, :, :], 0.0).then_inc(s_zero, 1)
            pool.wait_ge(s_eps, 2)
            pool.wait_ge(s_const, 16 * 7)
            with pool.Fori(0, ITERS) as it:
                zb = it * 11
                pool.wait_ge(s_vst, ONE + it * 16 + 16)
                for k in range(10):
                    v = n_t[:].rearrange("p (a s w) -> p a s w", s=2, w=1 << k)
                    if k:
                        pool.wait_ge(s_z, zb + k)
                    P.tensor_tensor(v[:, :, 1, :], v[:, :, 1, :], v[:, :, 0, :], ALU.add).then_inc(s_z, 1)
                pool.wait_ge(s_z, zb + 10)
                pool.wait_ge(s_full, ONE + it * SUNITS + SUNITS)
                P.tensor_tensor(k_t[:].rearrange("p (j l) -> p j l", l=LO),
                                n_t[:, SEQ - 1:SEQ].unsqueeze(2).broadcast_to([128, BLOCKS, LO]),
                                n_t[:].rearrange("p (l j) -> p j l", l=LO)[:, ::-1, ::-1], ALU.subtract)\
                    .then_inc(s_z, 1)
                pool.wait_ge(s_e0, it + 1)
                pool.wait_ge(s_z, zb + 11)
                P.tensor_tensor(n_t[:], k_t[:], n_t[:], ALU.mult).then_inc(s_ec, 1)
                base = it * len(LOWP)
                pool.wait_ge(s_mbe, it + 1)
                for k, (u, col, off, n, rs) in enumerate(LOWP):
                    if k == 0 or LOWP[k - 1][0] != u:
                        pool.wait_ge(s_exp, it * SUNITS + u + 1)
                    if k:
                        pool.wait_ge(s_den, base + k)
                    s = view_block(score[:, col + off:col + off + n], rs)
                    r = view_queries(q_t[:], rs)
                    if k == 0:
                        P.tensor_tensor(r, s, one[:].broadcast_to([128, n]), ALU.mult).then_inc(s_den, 1)
                    else:
                        P.tensor_tensor(r, r, s, ALU.add).then_inc(s_den, 1)


def _constants():
    import numpy as np
    pos = np.arange(SEQ)
    level = np.frexp((pos + 1).astype(np.float64))[1] - 1
    coord = (pos >> level) / 2.0 ** level
    div = np.exp(np.arange(0, D, 2, dtype=np.float64) * -(np.log(10000.0) / D))
    ang = pos[:, None].astype(np.float64) * div[None, :]
    pe = np.zeros((SEQ, D), np.float32)
    pe[:, 0::2] = (np.sin(ang) * coord[:, None]).astype(np.float32)
    pe[:, 1::2] = (np.cos(ang) * coord[:, None]).astype(np.float32)
    p = np.arange(128)
    lo = np.arange(LO)
    queries = np.arange(SEQ)
    allowed = np.array([1 << (10 - bin(int(i)).count("1")) for i in queries])
    floor = np.zeros((128, 1), np.float32)
    floor[0] = -3e38
    expert = np.arange(EXPERTS)
    chunk = np.arange(MCH - 1)
    ind = expert[:, None, None] == 2 * chunk[None, :, None] + (p // EF)[None, None, :]
    return {
        "pe_t": np.ascontiguousarray(pe.T),
        "ident": np.eye(128, dtype=np.float32),
        "sel": (p[:, None] // LO == np.arange(HEADS)[None, :]).astype(np.float32),
        "mean": np.full((128, 128), 1.0 / D, np.float32),
        "neg": np.where((p[:, None] % LO) & lo[None, :], np.float32(NEG), np.float32(0)).astype(np.float32),
        "cnt": (SEQ - allowed).astype(np.float32).reshape(SEQ // 128, 128).T,
        "floor": floor,
        "ind": np.tile(ind.astype(np.float32), (PARTS, 1, 1)),
    }


def kernel(**inputs):
    import numpy as np
    import concourse.bacc as bacc
    from concourse.bass_utils import run_bass_kernel_spmd

    a = {k: np.asarray(v) for k, v in inputs.items()}
    at = {k[8:]: v for k, v in a.items() if k.startswith("L0_attn_")}
    ff = {k[7:]: v for k, v in a.items() if k.startswith("L0_ffn_")}
    col = lambda v: v.reshape(LAYERS, D, 1)
    const = _constants()
    arrays = {
        "x_t": at["x"].transpose(0, 2, 1),
        "pe_t": const["pe_t"],
        "wa": np.concatenate([at["Wq"], at["Wk"], at["Wv"], col(at["bq"]), col(at["bk"]), col(at["bv"])], axis=2),
        "wb": np.concatenate(
            [at["Wo"], at["W1"], at["W2"].reshape(LAYERS, FCH, D, D).transpose(0, 2, 1, 3).reshape(LAYERS, D, HID)]
            + [col(at[k]) for k in ("bo", "b2", "ln1_g", "ln1_b", "ln2_g", "ln2_b")]
            + [at["b1"].reshape(LAYERS, FCH, D).transpose(0, 2, 1)], axis=2),
        "lnf": np.stack([at["lnf_g"], at["lnf_b"]], axis=1),
        "c_t": a["L0_c"].T,
        "wmod": a["L0_wmod"],
        "w_gate": ff["w_gate"].T,
        "we1": np.concatenate([ff["w1_e"].reshape(EXPERTS * EF, D), ff["w1_s"]]).T.reshape(D, MCH, 128),
        "we3": np.concatenate([ff["w3_e"].reshape(EXPERTS * EF, D), ff["w3_s"]]).T.reshape(D, MCH, 128),
        "we2": np.concatenate([ff["w2_e"].transpose(0, 2, 1).reshape(EXPERTS * EF, D), ff["w2_s"].T])
        .reshape(MCH, 128, D).transpose(1, 0, 2),
        "ident": const["ident"], "sel": const["sel"], "mean": const["mean"], "neg": const["neg"],
        "cnt": const["cnt"], "floor": const["floor"], "ind": const["ind"],
    }
    nc = bacc.Bacc("TRN2", target_bir_lowering=False, num_devices=1)
    feed, args = {}, []
    for name, v in arrays.items():
        feed[f"in_{name}"] = np.ascontiguousarray(v)
        args.append(nc.dram_tensor(f"in_{name}", v.shape, F32, kind="ExternalInput").ap())
    h_dram = nc.dram_tensor("h_scratch", (BATCH + ITERS, D, SEQ), F32, kind="Internal").ap()
    v_dram = nc.dram_tensor("v_scratch", (D, SEQ), F32, kind="Internal").ap()
    out = nc.dram_tensor("out_t", (BATCH, D, SEQ), F32, kind="ExternalOutput").ap()
    adaln_kernel(nc, *args, h_dram, v_dram, out)
    r = run_bass_kernel_spmd(nc, [feed], core_ids=[0])
    return np.ascontiguousarray(r.results[0]["out_t"].transpose(0, 2, 1))
```
